# Optimizing a Trainium2 kernel written in Bass

```python
import numpy as np
import jax
import jax.numpy as jnp

def _softmax(x, axis=-1):
    return jax.nn.softmax(x, axis=axis)

def _gelu(x):
    return jax.nn.gelu(x, approximate=True)

def _silu(x):
    return jax.nn.silu(x)

def _sigmoid(x):
    return jax.nn.sigmoid(x)

def _layernorm(x, axis=-1, eps=1e-05):
    m = jnp.mean(x, axis=axis, keepdims=True)
    v = jnp.var(x, axis=axis, keepdims=True)
    return (x - m) / jnp.sqrt(v + eps)

def _scatter_add(tgt, idx, src, axis=0):
    return tgt.at[idx].add(src)

def _segment_sum(src, seg, n):
    return jax.ops.segment_sum(src, seg, n)
kernel_name = 'mk_hybrid_d1_jaxref_r8_fc9cd8'

def setup_inputs(seed: int=0):
    np.random.seed(seed)
    _w = jnp.asarray

    def _L0_attn_a_setup():
        import jax, jax.numpy as jnp
        import numpy as np
        N_HEADS = 16
        N_KV_HEADS = 4
        HEAD_DIM = 128
        D_MODEL = 256
        SINK = 4
        WINDOW = 32
        B, T = (2, 256)

        def _sink_window_mask(t: int) -> jnp.ndarray:
            pos = jnp.arange(t)
            q = pos[:, None]
            k = pos[None, :]
            return (k <= q) & ((k < SINK) | (k >= q - WINDOW + 1))

        def _masked_softmax(scores: jnp.ndarray, mask: jnp.ndarray) -> jnp.ndarray:
            floor = jnp.finfo(scores.dtype).min
            ms = jnp.where(mask, scores, floor)
            row_max = jnp.max(ms, axis=-1, keepdims=True)
            row_max = jnp.where(jnp.isfinite(row_max), row_max, jnp.zeros_like(row_max))
            ex = jnp.exp(ms - row_max) * mask.astype(scores.dtype)
            denom = jnp.maximum(jnp.sum(ex, axis=-1, keepdims=True), 1e-09)
            return ex / denom
        key = jax.random.key(seed)
        k0, k1, k2, k3, k4 = jax.random.split(key, 5)
        s = 1.0 / np.sqrt(D_MODEL)
        return {'x': jax.random.normal(k0, (B, T, D_MODEL), dtype=jnp.float32), 'wq': jax.random.normal(k1, (N_HEADS * HEAD_DIM, D_MODEL), dtype=jnp.float32) * s, 'wk': jax.random.normal(k2, (N_KV_HEADS * HEAD_DIM, D_MODEL), dtype=jnp.float32) * s, 'wv': jax.random.normal(k3, (N_KV_HEADS * HEAD_DIM, D_MODEL), dtype=jnp.float32) * s, 'wo': jax.random.normal(k4, (D_MODEL, N_HEADS * HEAD_DIM), dtype=jnp.float32) * s}
    _L0_attn_a_in = _L0_attn_a_setup()

    def _L0_attn_b_setup():
        import jax, jax.numpy as jnp
        import numpy as np
        DIM = 256
        DIM_INNER = 512
        D_STATE = 64
        D_CONV = 4
        HEADDIM = 128
        NHEADS = DIM_INNER // HEADDIM
        CHUNK = 32
        BATCH = 1
        SEQ = 256
        CONV_DIM = DIM_INNER + 2 * D_STATE
        D_IN_PROJ = 2 * DIM_INNER + 2 * D_STATE + NHEADS

        def _segsum(a):
            T = a.shape[-1]
            cs = jnp.cumsum(a, axis=-1)
            seg = cs[..., :, None] - cs[..., None, :]
            mask = jnp.tril(jnp.ones((T, T), bool))
            return jnp.where(mask, seg, -jnp.inf)

        def _ssd(x, A, Bm, Cm, chunk):
            b, l, h, p = x.shape
            n = Bm.shape[-1]
            c = l // chunk
            x = x.reshape(b, c, chunk, h, p)
            A = A.reshape(b, c, chunk, h).transpose(0, 3, 1, 2)
            Bm = Bm.reshape(b, c, chunk, n)
            Cm = Cm.reshape(b, c, chunk, n)
            A_cumsum = jnp.cumsum(A, axis=-1)
            Lmat = jnp.exp(_segsum(A))
            Y_diag = jnp.einsum('bcln,bcsn,bhcls,bcshp->bclhp', Cm, Bm, Lmat, x)
            decay_states = jnp.exp(A_cumsum[..., -1:] - A_cumsum)
            states = jnp.einsum('bcln,bhcl,bclhp->bchpn', Bm, decay_states, x)
            states = jnp.concatenate([jnp.zeros_like(states[:, :1]), states], axis=1)
            A_last = jnp.pad(A_cumsum[..., -1], ((0, 0), (0, 0), (1, 0)))
            decay_chunk = jnp.exp(_segsum(A_last))
            new_states = jnp.einsum('bhzc,bchpn->bzhpn', decay_chunk, states)
            states, final_state = (new_states[:, :-1], new_states[:, -1])
            state_decay_out = jnp.exp(A_cumsum)
            Y_off = jnp.einsum('bcln,bchpn,bhcl->bclhp', Cm, states, state_decay_out)
            return ((Y_diag + Y_off).reshape(b, l, h, p), final_state)
        key = jax.random.key(seed)
        ks = jax.random.split(key, 8)
        x = jax.random.normal(ks[0], (BATCH, SEQ, DIM), jnp.float32)
        in_proj_w = jax.random.normal(ks[1], (D_IN_PROJ, DIM), jnp.float32) * 0.02
        conv_w = jax.random.normal(ks[2], (CONV_DIM, D_CONV), jnp.float32) * 0.2
        conv_b = jnp.zeros((CONV_DIM,), jnp.float32)
        dt_bias = jax.random.normal(ks[3], (NHEADS,), jnp.float32) * 0.1
        A_log = jnp.log(jax.random.uniform(ks[4], (NHEADS,), jnp.float32, 1.0, 16.0))
        D = jnp.ones((NHEADS,), jnp.float32)
        norm_w = jnp.ones((DIM_INNER,), jnp.float32)
        out_proj_w = jax.random.normal(ks[5], (DIM, DIM_INNER), jnp.float32) * 0.02
        return dict(x=x, in_proj_w=in_proj_w, conv_w=conv_w, conv_b=conv_b, dt_bias=dt_bias, A_log=A_log, D=D, norm_w=norm_w, out_proj_w=out_proj_w)
    _L0_attn_b_in = _L0_attn_b_setup()

    def _L0_ffn_setup():
        import jax, jax.numpy as jnp
        import numpy as np
        NUM_EXPERTS = 8
        TOP_K = 2
        LORA_ALPHA = 2.0
        LORA_RANK = 16
        D_MODEL = 256
        D_HIDDEN = 704
        key = jax.random.key(seed)
        ks = jax.random.split(key, 11)
        B, S, D, H, E, R = (2, 128, D_MODEL, D_HIDDEN, NUM_EXPERTS, LORA_RANK)
        sd = 1.0 / np.sqrt(D)
        sh = 1.0 / np.sqrt(H)
        x = jax.random.normal(ks[0], (B, S, D), jnp.float32)
        gate_w = jax.random.normal(ks[1], (E, D), jnp.float32) * sd
        w_up = jax.random.normal(ks[2], (H, D), jnp.float32) * sd
        w_gate = jax.random.normal(ks[3], (H, D), jnp.float32) * sd
        w_down = jax.random.normal(ks[4], (D, H), jnp.float32) * sh
        up_A = jax.random.normal(ks[5], (E, R, D), jnp.float32) * sd
        up_B = jax.random.normal(ks[6], (E, H, R), jnp.float32) * 0.02
        gate_A = jax.random.normal(ks[7], (E, R, D), jnp.float32) * sd
        gate_B = jax.random.normal(ks[8], (E, H, R), jnp.float32) * 0.02
        down_A = jax.random.normal(ks[9], (E, R, H), jnp.float32) * sh
        down_B = jax.random.normal(ks[10], (E, D, R), jnp.float32) * 0.02
        return {'x': x, 'gate_w': gate_w, 'w_up': w_up, 'w_gate': w_gate, 'w_down': w_down, 'up_A': up_A, 'up_B': up_B, 'gate_A': gate_A, 'gate_B': gate_B, 'down_A': down_A, 'down_B': down_B}
    _L0_ffn_in = _L0_ffn_setup()
    _d = {'L0_attn_a_x': _L0_attn_a_in['x'], 'L0_attn_a_wq': _L0_attn_a_in['wq'], 'L0_attn_a_wk': _L0_attn_a_in['wk'], 'L0_attn_a_wv': _L0_attn_a_in['wv'], 'L0_attn_a_wo': _L0_attn_a_in['wo'], 'L0_attn_b_in_proj_w': _L0_attn_b_in['in_proj_w'], 'L0_attn_b_conv_w': _L0_attn_b_in['conv_w'], 'L0_attn_b_conv_b': _L0_attn_b_in['conv_b'], 'L0_attn_b_dt_bias': _L0_attn_b_in['dt_bias'], 'L0_attn_b_A_log': _L0_attn_b_in['A_log'], 'L0_attn_b_D': _L0_attn_b_in['D'], 'L0_attn_b_norm_w': _L0_attn_b_in['norm_w'], 'L0_attn_b_out_proj_w': _L0_attn_b_in['out_proj_w'], 'L0_ffn_gate_w': _L0_ffn_in['gate_w'], 'L0_ffn_w_up': _L0_ffn_in['w_up'], 'L0_ffn_w_gate': _L0_ffn_in['w_gate'], 'L0_ffn_w_down': _L0_ffn_in['w_down'], 'L0_ffn_up_A': _L0_ffn_in['up_A'], 'L0_ffn_up_B': _L0_ffn_in['up_B'], 'L0_ffn_gate_A': _L0_ffn_in['gate_A'], 'L0_ffn_gate_B': _L0_ffn_in['gate_B'], 'L0_ffn_down_A': _L0_ffn_in['down_A'], 'L0_ffn_down_B': _L0_ffn_in['down_B']}
    _x0 = _d['L0_attn_a_x']
    _d['L0_attn_a_x'] = jax.random.normal(jax.random.fold_in(jax.random.key(seed), 1), (1, 1024, 256), dtype=_x0.dtype)
    del _x0
    return _d

def reference(L0_attn_a_x, L0_attn_a_wq, L0_attn_a_wk, L0_attn_a_wv, L0_attn_a_wo, L0_attn_b_in_proj_w, L0_attn_b_conv_w, L0_attn_b_conv_b, L0_attn_b_dt_bias, L0_attn_b_A_log, L0_attn_b_D, L0_attn_b_norm_w, L0_attn_b_out_proj_w, L0_ffn_gate_w, L0_ffn_w_up, L0_ffn_w_gate, L0_ffn_w_down, L0_ffn_up_A, L0_ffn_up_B, L0_ffn_gate_A, L0_ffn_gate_B, L0_ffn_down_A, L0_ffn_down_B):

    def _L0_attn_a_ref(x, wq, wk, wv, wo):
        import jax, jax.numpy as jnp
        import numpy as np
        N_HEADS = 16
        N_KV_HEADS = 4
        HEAD_DIM = 128
        D_MODEL = 256
        SINK = 4
        WINDOW = 32
        B, T = (2, 256)

        def _sink_window_mask(t: int) -> jnp.ndarray:
            pos = jnp.arange(t)
            q = pos[:, None]
            k = pos[None, :]
            return (k <= q) & ((k < SINK) | (k >= q - WINDOW + 1))

        def _masked_softmax(scores: jnp.ndarray, mask: jnp.ndarray) -> jnp.ndarray:
            floor = jnp.finfo(scores.dtype).min
            ms = jnp.where(mask, scores, floor)
            row_max = jnp.max(ms, axis=-1, keepdims=True)
            row_max = jnp.where(jnp.isfinite(row_max), row_max, jnp.zeros_like(row_max))
            ex = jnp.exp(ms - row_max) * mask.astype(scores.dtype)
            denom = jnp.maximum(jnp.sum(ex, axis=-1, keepdims=True), 1e-09)
            return ex / denom
        b, t, _ = x.shape
        group = N_HEADS // N_KV_HEADS
        q = (x @ wq.T).reshape(b, t, N_HEADS, HEAD_DIM).transpose(0, 2, 1, 3)
        k = (x @ wk.T).reshape(b, t, N_KV_HEADS, HEAD_DIM).transpose(0, 2, 1, 3)
        v = (x @ wv.T).reshape(b, t, N_KV_HEADS, HEAD_DIM).transpose(0, 2, 1, 3)
        k_full = jnp.repeat(k, group, axis=1)
        v_full = jnp.repeat(v, group, axis=1)
        scores = jnp.einsum('bhtd,bhsd->bhts', q, k_full) / np.sqrt(HEAD_DIM)
        mask = _sink_window_mask(t)[None, None, :, :]
        attn = _masked_softmax(scores.astype(jnp.float32), mask).astype(x.dtype)
        out = jnp.einsum('bhts,bhsd->bhtd', attn, v_full)
        out = out.transpose(0, 2, 1, 3).reshape(b, t, N_HEADS * HEAD_DIM)
        return out @ wo.T

    def _L0_attn_b_ref(x, in_proj_w, conv_w, conv_b, dt_bias, A_log, D, norm_w, out_proj_w):
        import jax, jax.numpy as jnp
        import numpy as np
        DIM = 256
        DIM_INNER = 512
        D_STATE = 64
        D_CONV = 4
        HEADDIM = 128
        NHEADS = DIM_INNER // HEADDIM
        CHUNK = 32
        BATCH = 1
        SEQ = 256
        CONV_DIM = DIM_INNER + 2 * D_STATE
        D_IN_PROJ = 2 * DIM_INNER + 2 * D_STATE + NHEADS

        def _segsum(a):
            T = a.shape[-1]
            cs = jnp.cumsum(a, axis=-1)
            seg = cs[..., :, None] - cs[..., None, :]
            mask = jnp.tril(jnp.ones((T, T), bool))
            return jnp.where(mask, seg, -jnp.inf)

        def _ssd(x, A, Bm, Cm, chunk):
            b, l, h, p = x.shape
            n = Bm.shape[-1]
            c = l // chunk
            x = x.reshape(b, c, chunk, h, p)
            A = A.reshape(b, c, chunk, h).transpose(0, 3, 1, 2)
            Bm = Bm.reshape(b, c, chunk, n)
            Cm = Cm.reshape(b, c, chunk, n)
            A_cumsum = jnp.cumsum(A, axis=-1)
            Lmat = jnp.exp(_segsum(A))
            Y_diag = jnp.einsum('bcln,bcsn,bhcls,bcshp->bclhp', Cm, Bm, Lmat, x)
            decay_states = jnp.exp(A_cumsum[..., -1:] - A_cumsum)
            states = jnp.einsum('bcln,bhcl,bclhp->bchpn', Bm, decay_states, x)
            states = jnp.concatenate([jnp.zeros_like(states[:, :1]), states], axis=1)
            A_last = jnp.pad(A_cumsum[..., -1], ((0, 0), (0, 0), (1, 0)))
            decay_chunk = jnp.exp(_segsum(A_last))
            new_states = jnp.einsum('bhzc,bchpn->bzhpn', decay_chunk, states)
            states, final_state = (new_states[:, :-1], new_states[:, -1])
            state_decay_out = jnp.exp(A_cumsum)
            Y_off = jnp.einsum('bcln,bchpn,bhcl->bclhp', Cm, states, state_decay_out)
            return ((Y_diag + Y_off).reshape(b, l, h, p), final_state)
        B, L, _ = x.shape
        zxbcdt = x @ in_proj_w.T
        z = zxbcdt[..., :DIM_INNER]
        xBC = zxbcdt[..., DIM_INNER:DIM_INNER + CONV_DIM]
        dt = jax.nn.softplus(zxbcdt[..., -NHEADS:] + dt_bias)
        xc = xBC.transpose(0, 2, 1)
        xc = jax.lax.conv_general_dilated(xc, conv_w[:, None, :], (1,), [(D_CONV - 1, 0)], dimension_numbers=('NCH', 'OIH', 'NCH'), feature_group_count=CONV_DIM)
        xc = xc + conv_b[None, :, None]
        xBC = jax.nn.silu(xc).transpose(0, 2, 1)
        xs = xBC[..., :DIM_INNER].reshape(B, L, NHEADS, HEADDIM)
        Bmat = xBC[..., DIM_INNER:DIM_INNER + D_STATE]
        Cmat = xBC[..., DIM_INNER + D_STATE:]
        A = -jnp.exp(A_log)
        y, final_state = _ssd(xs * dt[..., None], A * dt, Bmat, Cmat, CHUNK)
        y = y + xs * D[:, None]
        y = y.reshape(B, L, DIM_INNER)
        g = y * jax.nn.silu(z)
        g = g * jax.lax.rsqrt(jnp.mean(g * g, axis=-1, keepdims=True) + 1e-05) * norm_w
        return g @ out_proj_w.T

    def _L0_ffn_ref(x, gate_w, w_up, w_gate, w_down, up_A, up_B, gate_A, gate_B, down_A, down_B):
        import jax, jax.numpy as jnp
        import numpy as np
        NUM_EXPERTS = 8
        TOP_K = 2
        LORA_ALPHA = 2.0
        LORA_RANK = 16
        D_MODEL = 256
        D_HIDDEN = 704
        B, S, D = x.shape
        H = w_up.shape[0]
        gate_logits = jnp.einsum('bsd,ed->bse', x, gate_w)
        topw, sel = jax.lax.top_k(gate_logits, TOP_K)
        topw = jax.nn.softmax(topw.astype(jnp.float32), axis=1).astype(x.dtype)
        xt = x.reshape(-1, D)
        wf = topw.reshape(-1, TOP_K)
        sf = sel.reshape(-1, TOP_K)
        base_up = xt @ w_up.T
        base_gate = xt @ w_gate.T
        mixed_h = jnp.zeros((xt.shape[0], H), x.dtype)
        lora_down = jnp.zeros_like(xt)
        for e in range(NUM_EXPERTS):
            c = jnp.sum(jnp.where(sf == e, wf, 0.0), axis=1)
            lo_up = LORA_ALPHA * (xt @ up_A[e].T @ up_B[e].T)
            lo_gate = LORA_ALPHA * (xt @ gate_A[e].T @ gate_B[e].T)
            h_e = jax.nn.silu(base_up + lo_up) * (base_gate + lo_gate)
            ch = c[:, None] * h_e
            mixed_h = mixed_h + ch
            lora_down = lora_down + LORA_ALPHA * (ch @ down_A[e].T @ down_B[e].T)
        out = mixed_h @ w_down.T + lora_down
        return out.reshape(B, S, D)
    x = L0_attn_a_x
    x = x + _L0_attn_a_ref(_layernorm(x, axis=-1), L0_attn_a_wq, L0_attn_a_wk, L0_attn_a_wv, L0_attn_a_wo)
    x = x + _L0_ffn_ref(_layernorm(x, axis=-1), L0_ffn_gate_w, L0_ffn_w_up, L0_ffn_w_gate, L0_ffn_w_down, L0_ffn_up_A, L0_ffn_up_B, L0_ffn_gate_A, L0_ffn_gate_B, L0_ffn_down_A, L0_ffn_down_B)
    x = x + _L0_attn_b_ref(_layernorm(x, axis=-1), L0_attn_b_in_proj_w, L0_attn_b_conv_w, L0_attn_b_conv_b, L0_attn_b_dt_bias, L0_attn_b_A_log, L0_attn_b_D, L0_attn_b_norm_w, L0_attn_b_out_proj_w)
    x = x + _L0_ffn_ref(_layernorm(x, axis=-1), L0_ffn_gate_w, L0_ffn_w_up, L0_ffn_w_gate, L0_ffn_w_down, L0_ffn_up_A, L0_ffn_up_B, L0_ffn_gate_A, L0_ffn_gate_B, L0_ffn_down_A, L0_ffn_down_B)
    return x

_drawn_inputs = setup_inputs


def setup_inputs(seed=0):
    import zlib

    import numpy as np

    out = dict(_drawn_inputs(seed))
    spreads = {'L0_attn_b_conv_b': (0.0, 0.1), 'L0_attn_b_D': (1.0, 0.2), 'L0_attn_b_norm_w': (1.0, 0.2)}
    factors = {'L0_attn_b_dt_bias': 27.109,
     'L0_attn_b_A_log': 8.0,
     'L0_ffn_gate_w': 5.125,
     'L0_ffn_w_up': 4.011,
     'L0_ffn_w_gate': 3.74,
     'L0_ffn_w_down': 3.579,
     'L0_ffn_up_A': 8.0,
     'L0_ffn_up_B': 8.0,
     'L0_ffn_gate_A': 8.0,
     'L0_ffn_gate_B': 8.0,
     'L0_ffn_down_A': 8.0,
     'L0_ffn_down_B': 8.0}
    for name, (base, spread) in spreads.items():
        noise = np.random.default_rng([zlib.crc32(name.encode()), seed]).standard_normal(out[name].shape)
        drawn = base * np.exp(spread * noise) if base else spread * noise
        out[name] = jnp.asarray(drawn.astype(out[name].dtype))
    for name, factor in factors.items():
        out[name] = (out[name] * factor).astype(out[name].dtype)
    return out
```

```python
from contextlib import ExitStack

import numpy as np

import concourse.bass as bass
from concourse import mybir

F32 = mybir.dt.float32
F32R = mybir.dt.float32r
BF16 = mybir.dt.bfloat16
U16 = mybir.dt.uint16
U32 = mybir.dt.uint32
ALU = mybir.AluOpType
ACT = mybir.ActivationFunctionType
AX = mybir.AxisListType

P = 128
T = 1024
NT = T // P
D = 256
KB = D // P
HALF = T // 2
HT = NT // 2
HI, LO = 0, 1
TERMS = ((HI, HI), (HI, LO), (LO, HI))
LN_EPS = 1e-5
MASKED = -1e30

HEADS, KV, HD = 16, 4, 128
GROUP = HEADS // KV
SINK, WINDOW = 4, 32
QT_LEN = 90
KWIN = QT_LEN + WINDOW
NKEY = SINK + KWIN
NJ = 1 + -(-(T - P) // QT_LEN)
Q0 = [0] + [P + QT_LEN * j for j in range(NJ - 1)]
QN = [P] + [min(QT_LEN, T - q) for q in Q0[1:]]
NK = [P] + [NKEY] * (NJ - 1)
KOFF = [0] + [P + NKEY * j for j in range(NJ - 1)]
W0 = Q0[1] - WINDOW
WLAST = T - (W0 + QT_LEN * (NJ - 2))
TPAD = W0 + QT_LEN * (NJ - 2) + KWIN
KTL = P + NKEY * (NJ - 1)

EXPERTS, RANK, HID = 8, 16, 704
ER = EXPERTS * RANK
HB = -(-HID // P)
HIDP = HB * P
ALPHA = 2.0
SLOTS = 2

INNER, NH, STATE, CONV = 512, 4, 64, 4
CB = 6
INP_COLS = INNER + INNER + 2 * P

C_ID, C_AFTER, C_UPTO, C_ONES = (P * i for i in range(4))
B_ID, B_ECOL, B_M0 = 0, P, 2 * P
B_M1 = B_M0 + GROUP * P
B_END = B_M1 + GROUP * NKEY
PR_CW, PR_CB, PR_NW, PR_D, PR_DTB, PR_AL, PR_GW = 0, 24, 30, 34, 38, 42, 46
PR_END = PR_GW + KB * EXPERTS
GW_PARTS = 2 * KB * EXPERTS
GW_PAD = GW_PARTS - EXPERTS + P
F_UPA, F_GTA, F_BLK = 0, KB * P, 2 * KB * P
FB_UP, FB_GT, FB_UPB, FB_GTB = 0, KB * P, 2 * KB * P, 2 * KB * P + P
FB_DN = FB_GTB + P
FB_DA = FB_DN + D
FB = FB_DA + ER
F_DB = F_BLK + HB * FB
F_END = F_DB + D
F_CUTS = [0] + [F_BLK + b * FB for b in range(HB + 1)] + [F_END]
M_IN, M_OUT = 0, KB * INP_COLS
M_END = M_OUT + NH * D
M_CUTS = [0, 2 * KB * P, 6 * KB * P, M_OUT, M_END]


def build(nc, ins, out, phases=4):
    ctx = ExitStack()
    with ctx:
        def sem(name):
            return ctx.enter_context(nc.semaphore(name))

        base = [16512]

        def keep(name, shape, dt):
            size = int(np.prod(shape[1:])) * (2 if dt in (BF16, U16) else 4)
            t = nc.alloc_sbuf_tensor_at(name, shape, dt, offset=base[0])
            base[0] += -(-size // 32) * 32
            return t

        def at(name, shape, dt, offset):
            return nc.alloc_sbuf_tensor_at(name, shape, dt, offset=offset)

        cf_all = keep("const_f32", [P, 4 * P], F32)
        cf = cf_all[:, :]
        gw_hl = keep("router_w_hl", [P, GW_PAD], F32R)
        cb_bits = keep("const_bf16_bits", [P, B_END], U16)
        cb = cb_bits[:, :].bitcast(BF16)
        par = keep("params", [P, PR_END], F32)
        x = keep("x_resid", [P, NT, D], F32)
        stats = keep("ln_stats", [P, NT, 6], F32)
        mv = keep("ln_mean_var", [P, NT, 2], F32)
        veps = keep("ln_var_eps", [P, NT], F32)
        rstd = keep("ln_rstd", [P, NT], F32)
        minus_half = keep("minus_half", [P, NT], F32)
        small = keep("small", [P, 256], F32)
        sm = keep("softmax_small", [P, 48], F32)
        R = base[0]
        A_X = R
        A_V = A_X + 2 * KB * TPAD * 4
        A_K = A_V + 2 * NJ * KV * HD * 4
        A_W = -(-(A_K + KV * KTL * 4) // 32) * 32
        A_Q = A_W + 32768
        A_O = A_Q + 16384
        A_P = A_O + 32768
        A_WO = A_P + 14336
        END = A_WO + 16384
        assert END <= 229344, END

        ident = cf[:, C_ID:C_ID + P]
        identb = cb[:, B_ID:B_ID + P]
        ones = cf[:, C_ONES:C_ONES + P]

        PS = ctx.enter_context(nc.psum_tensor("psum", [P, 8, 512], F32))

        def bank(i):
            return PS[:, i, :]

        xT = at("xT_hl", [P, 2, KB, TPAD], F32R, A_X)
        xn_in_xT = at("xn", [P, 2, KB, TPAD], F32, A_X)

        def f32(ap):
            return ap.bitcast(F32)

        def three(e, dst, lhs, rhs, start, stop, **kw):
            for n, (a, b) in enumerate(TERMS):
                i = e.matmul(dst, lhs(a), rhs(b), start=start and n == 0,
                             stop=stop and n == len(TERMS) - 1, **kw)
            return i

        def spread(ap, n):
            return ap.rearrange("p (a o) -> p a o", o=1).broadcast_to([ap.shape[0], ap.shape[1], n])

        def repeat(ap, n):
            return ap.rearrange("p (o a) -> p o a", o=1).broadcast_to([ap.shape[0], n, ap.shape[1]])

        s_x = [sem("x_half0"), sem("x_half1")]
        s_cf, s_cb, s_par, s_out = sem("const_f32_in"), sem("const_bf16_in"), sem("params_in"), sem("out_stored")
        s_init, s_gwh, s_gwl = sem("init"), sem("router_w_hi"), sem("router_w_lo")

        LN_EVENTS = dict(stats=NT, aggr=NT, veps=2, rstd=2, xn=NT, tr=2, hi=2 * KB, lo=2 * KB)
        LN = {n: sem(f"ln_{n}") for n in LN_EVENTS}
        ln_turns = list(range(4))

        def layer_norm(x_ready, xt_free, banks, banks_free):
            turn = ln_turns.pop(0)

            def xn(t):
                h, i = divmod(t, HT)
                return xn_in_xT[:, i // KB, i % KB, HALF * h:HALF * h + D]

            def need(e, name, n):
                e.wait_ge(LN[name], turn * LN_EVENTS[name] + n)

            def stats_dve(e, *tiles):
                for t in tiles:
                    x_ready(e, t)
                    e.bn_stats(stats[:, t, :], x[:, t, :]).then_inc(LN["stats"], 1)
                for t in tiles:
                    need(e, "stats", t + 1)
                    e.bn_aggr(mv[:, t, :], stats[:, t, :]).then_inc(LN["aggr"], 1)

            def veps_dve(e, h):
                need(e, "aggr", HT * (h + 1))
                e.tensor_scalar(veps[:, HT * h:HT * h + HT], mv[:, HT * h:HT * h + HT, 1], LN_EPS, None,
                                ALU.add).then_inc(LN["veps"], 1)

            def rstd_pool(e, h):
                e.wait_ge(s_init, 1)
                need(e, "veps", h + 1)
                seg = slice(HT * h, HT * h + HT)
                e.tensor_tensor(rstd[:, seg], veps[:, seg], minus_half[:, seg], ALU.pow).then_inc(LN["rstd"], 1)

            def norm_dve(e, h):
                xt_free(e, h)
                need(e, "rstd", h + 1)
                for t in range(HT * h, HT * h + HT):
                    e.tensor_scalar(xn(t), x[:, t, :], mv[:, t, 0:1], rstd[:, t:t + 1],
                                    ALU.subtract, ALU.mult).then_inc(LN["xn"], 1)

            def tr_pe(e, h):
                banks_free(e, h)
                for i in range(HT):
                    need(e, "xn", HT * h + i + 1)
                    for k in range(KB):
                        m = e.transpose(bank(banks[h][k])[:, i * P:(i + 1) * P],
                                        xn(HT * h + i)[:, k * P:(k + 1) * P], ident)
                m.then_inc(LN["tr"], 1)

            def hi_act(e, h):
                need(e, "tr", h + 1)
                for k in range(KB):
                    e.activation(xT[:, HI, k, HALF * h:HALF * h + HALF], bank(banks[h][k]),
                                 ACT.Copy).then_inc(LN["hi"], 1)

            def lo_dve(e, h):
                for k in range(KB):
                    need(e, "hi", 2 * h + k + 1)
                    seg = slice(HALF * h, HALF * h + HALF)
                    e.tensor_tensor(xT[:, LO, k, seg], bank(banks[h][k]), f32(xT[:, HI, k, seg]),
                                    ALU.subtract).then_inc(LN["lo"], 1)

            def ready(e, h=1):
                need(e, "lo", 2 * h + 2)

            return dict(stats=stats_dve, veps=veps_dve, rstd=rstd_pool, norm=norm_dve, tr=tr_pe, hi=hi_act, lo=lo_dve, ready=ready)

        def early_stages(ln):
            def queued(stage):
                return lambda e: ln[stage](e, 0)
            return {stage + "0": queued(stage) for stage in ("veps", "rstd", "norm", "tr", "hi", "lo")} | {"stats": ln["stats"]}

        def early(phase, stage, e, *args):
            if stage in phase["next"]:
                phase["next"][stage](e, *args)

        def attention():
            kT = at("kT", [P, KV, KTL], F32, A_K)
            v_hl = at("v_hl", [P, 2, NJ, KV * HD], F32R, A_V)
            wq_hl = at("wq_hl", [P, 2, 2, KB, HALF], F32R, A_W)
            raw = at("w_raw", [P, 4, 1024], F32, A_W + 16384)
            qT = at("qT", [P, GROUP, T], F32, A_Q)
            oT_hl = at("oT_hl", [P, 2, GROUP, T], F32R, A_O)
            xg_hl = at("xg_hl", [P, 2, KB, NJ - 1, NKEY], F32R, A_O)
            wk_hl = at("wk_hl", [P, 2, KB, KV * HD], F32R, A_O + 20480)
            wv_hl = at("wv_hl", [P, 2, KB, KV * HD], F32R, A_WO + 8192)
            wo_hl = at("wo_hl", [P, 2, 2, GROUP, D], F32R, A_WO)
            pr = at("probs", [P, 3, 512], F32, A_P)
            pT_hl = at("pT_hl", [P, 2, 2, 512], F32R, A_P + 6144)
            NEGM, DEN, DENG, RDEN = (small[:, 192 + 16 * i:208 + 16 * i].rearrange("p (b h) -> p b h", b=4) for i in range(4))

            s_raw = [sem(f"w_raw{n}") for n in range(4)]
            s_wh, s_wl = sem("att_w_hi"), sem("att_w_lo")
            s_pad, s_xg = sem("x_pad"), sem("xg")
            s_k, s_kev, s_v, s_vhi, s_vlo = sem("k_mm"), sem("k_ev"), sem("v_mm"), sem("v_hi"), sem("v_lo")
            s_q, s_qt, s_mask = sem("q_mm"), sem("q_ev"), sem("masked")
            s_s, s_max, s_exp, s_dg, s_rd, s_nrm = (sem(n) for n in ("scores", "rowmax", "expd", "den_guard", "recip", "normed"))
            s_t, s_phi, s_plo = sem("p_tr"), sem("pT_hi"), sem("pT_lo")
            s_o, s_ohi, s_olo = sem("o_mm"), sem("oT_hi"), sem("oT_lo")
            s_y, s_add = sem("y_mm"), sem("x_add")

            ln = layer_norm(lambda e, t: e.wait_ge(s_x[t // HT], 16), lambda e, h: None, ((0, 1), (2, 3)),
                            lambda e, h: None)
            phase = {"next": {}}
            units = [(g, j) for g in range(KV) for j in range(NJ)]
            NU = len(units)
            loads = ["wk", "wv", "wq0", "wo0", "wq1", "wo1", "wq2", "wo2", "wq3", "wo3"]
            parts = {"wk": wk_hl, "wv": wv_hl}
            for g in range(KV):
                parts[f"wq{g}"] = wq_hl[:, g % 2]
                parts[f"wo{g}"] = wo_hl[:, g % 2]
            WQ = [loads.index(f"wq{g}") + 1 for g in range(KV)]
            WO = [loads.index(f"wo{g}") + 1 for g in range(KV)]

            def part(n, which):
                return parts[loads[n]][:, which].rearrange("p a b -> p (a b)")

            LAG_T, LAG_P, LAG_O, LAG_F, LAG_Y = 2, 3, 4, 5, 6
            FIRST_UNITS = {NJ - 4: 0, NJ - 2: 1}
            q_chunk = {}
            for g in range(1, KV):
                for h in range(GROUP):
                    q_chunk[(g - 1) * NJ + 6 + h] = (g * 2 + 0) * GROUP + h
                    q_chunk[g * NJ + h] = (g * 2 + 1) * GROUP + h
            last_unit = [next(j for j in range(NJ) if Q0[j] + QN[j] >= (t + 1) * P) for t in range(NT)]
            y_tile = {g * NJ + last_unit[t] + LAG_Y: g * NT + t for g in range(KV) for t in range(NT)}
            assert len(y_tile) == KV * NT
            STEPS = max(y_tile) + 1
            w_step = {}
            for g in range(1, KV):
                if g > 1:
                    w_step[(g - 1) * NJ + 1] = WQ[g] - 1
                w_step[(g - 1) * NJ + (4 if g == 1 else 7)] = WO[g] - 1

            def weight_free(e, n):
                name, g = loads[n][:2], n
                if name == "wq" and n >= WQ[2] - 1:
                    g = WQ.index(n + 1)
                    e.wait_ge(s_q, (g - 1) * 2 * GROUP)
                if name == "wo":
                    g = WO.index(n + 1)
                    if g == 1:
                        e.wait_ge(s_v, NJ)
                    if g >= 2:
                        e.wait_ge(s_y, (g - 1) * NT)

            def sync(e):
                for n, name in enumerate(loads):
                    if n >= 4:
                        e.wait_ge(s_wl, n - 3)
                    src = {"wk": ins["wk"], "wv": ins["wv"]}.get(name)
                    if src is None:
                        src = ins[name[:2]][int(name[2])]
                    e.dma_start(raw[:, n % 4, :], src).then_inc(s_raw[n % 4], 16)
                    if n == 3:
                        e.dma_start(cb_bits[:, :], ins["cb"]).then_inc(s_cb, 16)
                        e.dma_start(par[:, :], ins["par"]).then_inc(s_par, 16)

            def w_hi(e, n):
                e.wait_ge(s_raw[n % 4], 16 * (n // 4 + 1))
                weight_free(e, n)
                e.activation(part(n, HI), raw[:, n % 4, :], ACT.Copy).then_inc(s_wh, 1)

            def w_lo(e, n):
                e.wait_ge(s_wh, n + 1)
                e.tensor_tensor(part(n, LO), raw[:, n % 4, :], f32(part(n, HI)), ALU.subtract).then_inc(s_wl, 1)

            def win(ap3, n):
                return bass.AP(ap3.tensor, ap3.offset + W0, [ap3.ap[0], (QT_LEN, n), (1, KWIN)])

            def gather(e, copy, which, k):
                src = xT[:, which, k, :]
                copy(xg_hl[:, which, k, :, SINK:NKEY], f32(win(src, NJ - 1)))
                return copy(xg_hl[:, which, k, :, 0:SINK], f32(repeat(xT[:, which, k, 0:SINK], NJ - 1)))

            def pe(e):
                e.wait_ge(s_cf, 16)
                for h in range(2):
                    ln["tr"](e, h)
                ln["ready"](e, 0)
                for g in range(KV):
                    if g == 0:
                        e.wait_ge(s_wl, 1)
                    if g >= 2:
                        e.wait_ge(s_kev, g - 1)
                    for h in range(2):
                        if g == 0 and h == 1:
                            ln["ready"](e, 1)
                        for k in range(KB):
                            m = three(e, bank(2 * (g % 2) + h), lambda w: wk_hl[:, w, k, g * HD:(g + 1) * HD],
                                      lambda w: xT[:, w, k, HALF * h:HALF * h + HALF], k == 0, k == KB - 1)
                    m.then_inc(s_k, 1)

                def queries(n):
                    g, h = n // (2 * GROUP), n % GROUP
                    half = n // GROUP % 2
                    e.wait_ge(s_wl, WQ[g])
                    if n:
                        e.wait_ge(s_qt, n)
                    for k in range(KB):
                        m = three(e, bank(6), lambda w: wq_hl[:, g % 2, w, k, h * HD:(h + 1) * HD],
                                  lambda w: xT[:, w, k, HALF * half:HALF * half + HALF], k == 0, k == KB - 1)
                    m.then_inc(s_q, 1)

                def scores(u):
                    g, j = units[u]
                    qn, nk = QN[j], NK[j]
                    if u == 0:
                        e.wait_ge(s_kev, KV)
                    if u >= 2:
                        e.wait_ge(s_mask, u - 1)
                    e.wait_ge(s_qt, g * 2 * GROUP + (GROUP if Q0[j] + qn <= HALF else 2 * GROUP))
                    dst = bank(u % 2)[0:qn, 0:GROUP * nk]
                    for h in range(GROUP):
                        m = e.matmul(dst[:, h * nk:(h + 1) * nk], qT[:, h, Q0[j]:Q0[j] + qn],
                                     kT[:, g, KOFF[j]:KOFF[j] + nk], start=True, stop=True)
                    m.then_inc(s_s, 1)

                for j in range(NJ):
                    if j in FIRST_UNITS:
                        scores(FIRST_UNITS[j])
                    if j == 0:
                        e.wait_ge(s_wl, 2)
                    if j == 1:
                        e.wait_ge(s_xg, 2 * KB)
                    if j >= 2:
                        e.wait_ge(s_vlo, j - 1)
                    for k in range(KB):
                        m = three(e, bank(4 + j % 2)[0:NK[j], :],
                                  lambda w: xT[:, w, k, 0:P] if j == 0 else xg_hl[:, w, k, j - 1, :],
                                  lambda w: wv_hl[:, w, k, :], k == 0, k == KB - 1)
                    m.then_inc(s_v, 1)
                    if j < 2 * GROUP:
                        queries(j)

                def p_transpose(u):
                    g, j = units[u]
                    qn, nk = QN[j], NK[j]
                    e.wait_ge(s_nrm, u + 1)
                    if u >= 2:
                        e.wait_ge(s_plo, u - 1)
                    for h in range(GROUP):
                        m = e.transpose(bank(2 + u % 2)[0:nk, h * qn:(h + 1) * qn],
                                        pr[0:qn, u % 3, h * nk:(h + 1) * nk], ident[0:qn, 0:qn])
                    m.then_inc(s_t, 1)

                def p_v(u):
                    g, j = units[u]
                    n = GROUP * QN[j]
                    e.wait_ge(s_plo, u + 1)
                    if u < 2:
                        e.wait_ge(s_vlo, NJ)
                    else:
                        e.wait_ge(s_olo, u - 1)
                    three(e, bank(4 + u % 2)[:, 0:n], lambda w: v_hl[0:NK[j], w, j, g * HD:(g + 1) * HD],
                          lambda w: pT_hl[0:NK[j], u % 2, w, 0:n], True, True).then_inc(s_o, 1)

                def project(n):
                    g, t = n // NT, n % NT
                    e.wait_ge(s_olo, g * NJ + last_unit[t] + 1)
                    e.wait_ge(s_wl, WO[g])
                    if n:
                        e.wait_ge(s_add, n)
                    for h in range(GROUP):
                        m = three(e, bank(7)[:, 0:D], lambda w: oT_hl[:, w, h, t * P:(t + 1) * P],
                                  lambda w: wo_hl[:, g % 2, w, h, :], h == 0, h == GROUP - 1)
                    m.then_inc(s_y, 1)

                for i in range(STEPS):
                    if len(FIRST_UNITS) <= i < NU:
                        scores(i)
                    if i in q_chunk:
                        queries(q_chunk[i])
                    if i == NU + 2:
                        early(phase, "tr0", e)
                    if i in y_tile:
                        project(y_tile[i])
                    if 0 <= i - LAG_O < NU:
                        p_v(i - LAG_O)
                    if 0 <= i - LAG_T < NU:
                        p_transpose(i - LAG_T)
                    if i == NU + 3:
                        early(phase, "logits0", e)
                    if i == NU + 4:
                        early(phase, "logits_tr0", e)
                early(phase, "lora_a0", e)
                early(phase, "base_x0", e)

            def act(e):
                w_hi(e, 0)
                w_hi(e, 1)
                w_hi(e, 2)
                for h in range(2):
                    ln["hi"](e, h)
                ln["ready"](e)
                e.wait_ge(s_pad, 1)
                for k in range(KB):
                    gather(e, lambda o, i: e.activation(o, i, ACT.Copy), HI, k).then_inc(s_xg, 1)

                def q_evac(n):
                    h, half, g = n % GROUP, n // GROUP % 2, n // (2 * GROUP)
                    e.wait_ge(s_q, n + 1)
                    if g and half == 0:
                        e.wait_ge(s_s, (g - 1) * NJ + 6)
                    if g and half == 1:
                        e.wait_ge(s_s, g * NJ)
                    e.activation(qT[:, h, HALF * half:HALF * half + HALF], bank(6), ACT.Copy,
                                 scale=float(HD) ** -0.5).then_inc(s_qt, 1)

                def exps(u):
                    g, j = units[u]
                    qn, nk = QN[j], NK[j]
                    e.wait_ge(s_max, u + 1)
                    if u >= 4:
                        e.wait_ge(s_rd, u - 3)
                    for h in range(GROUP):
                        m = e.activation(pr[0:qn, u % 3, h * nk:(h + 1) * nk], pr[0:qn, u % 3, h * nk:(h + 1) * nk],
                                         ACT.Exp, bias=NEGM[0:qn, u % 4, h:h + 1],
                                         accum_out=DEN[0:qn, u % 4, h:h + 1])
                    m.then_inc(s_exp, 1)

                w_hi(e, 3)
                w_hi(e, 4)
                for j in range(NJ):
                    if j in FIRST_UNITS:
                        exps(FIRST_UNITS[j])
                    e.wait_ge(s_v, j + 1)
                    e.activation(v_hl[0:NK[j], HI, j, :], bank(4 + j % 2)[0:NK[j], :], ACT.Copy).then_inc(s_vhi, 1)
                    if j < 2 * GROUP:
                        q_evac(j)
                e.wait_ge(s_par, 16)
                e.wait_ge(s_cf, 16)
                e.activation(gw_hl[:, GW_PARTS:], cf[:, 0:GW_PAD - GW_PARTS], ACT.Copy, scale=0.0)
                e.activation(gw_hl[:, 0:GW_PARTS // 2], par[:, PR_GW:PR_END], ACT.Copy).then_inc(s_gwh, 1)

                def pT_hi(u):
                    n, nk = GROUP * QN[units[u][1]], NK[units[u][1]]
                    e.wait_ge(s_t, u + 1)
                    if u >= 2:
                        e.wait_ge(s_o, u - 1)
                    e.activation(pT_hl[0:nk, u % 2, HI, 0:n], bank(2 + u % 2)[0:nk, 0:n], ACT.Copy).then_inc(s_phi, 1)

                def oT_hi(u):
                    g, j = units[u]
                    e.wait_ge(s_o, u + 1)
                    if g:
                        e.wait_ge(s_y, (g - 1) * NT + min(NT, -(-(Q0[j] + QN[j]) // P)))
                    e.activation(oT_hl[:, HI, :, Q0[j]:Q0[j] + QN[j]],
                                 bank(4 + u % 2)[:, 0:GROUP * QN[j]].rearrange("p (h q) -> p h q", h=GROUP),
                                 ACT.Copy).then_inc(s_ohi, 1)

                for i in range(STEPS):
                    if i in q_chunk:
                        q_evac(q_chunk[i])
                    if 0 <= i - LAG_P < NU:
                        pT_hi(i - LAG_P)
                    if 0 <= i - LAG_F < NU:
                        oT_hi(i - LAG_F)
                    if len(FIRST_UNITS) <= i < NU:
                        exps(i)
                    if i in w_step:
                        w_hi(e, w_step[i])
                    if i == NU + 2:
                        early(phase, "hi0", e)

            def dve(e):
                e.memset(f32(xT[:, :, :, T:TPAD]), 0.0).then_inc(s_pad, 1)
                for h in range(2):
                    ln["stats"](e, *range(HT * h, HT * h + HT))
                    ln["veps"](e, h)
                for h in range(2):
                    ln["norm"](e, h)
                for h in range(2):
                    ln["lo"](e, h)
                ln["ready"](e)
                e.wait_ge(s_pad, 1)
                for k in range(KB):
                    gather(e, e.tensor_copy, LO, k).then_inc(s_xg, 1)
                for g in range(KV):
                    e.wait_ge(s_k, g + 1)
                    b0 = 2 * (g % 2)
                    keys = PS[:, b0:b0 + 2, :].rearrange("p b n -> p (b n)")
                    full = NJ - 2
                    tiles = kT[:, g, P:KTL].rearrange("p (i c) -> p i c", c=NKEY)
                    e.tensor_copy(kT[:, g, 0:P], keys[:, 0:P])
                    e.tensor_copy(tiles[:, 0:full, SINK:NKEY], win(keys, full))
                    e.tensor_copy(tiles[:, full, SINK:SINK + WLAST], keys[:, T - WLAST:T])
                    e.memset(tiles[:, full, SINK + WLAST:NKEY], 0.0)
                    e.tensor_copy(tiles[:, :, 0:SINK], repeat(keys[:, 0:SINK], NJ - 1)).then_inc(s_kev, 1)
                def recip(u):
                    qn = QN[units[u][1]]
                    e.wait_ge(s_exp, u + 1)
                    if u >= 4:
                        e.wait_ge(s_nrm, u - 3)
                    e.tensor_scalar(DENG[0:qn, u % 4, :], DEN[0:qn, u % 4, :], 1e-9, None, ALU.max).then_inc(s_dg, 1)
                    e.wait_ge(s_dg, u + 1)
                    e.reciprocal(RDEN[0:qn, u % 4, :], DENG[0:qn, u % 4, :]).then_inc(s_rd, 1)

                def row_max(u):
                    g, j = units[u]
                    qn, nk = QN[j], NK[j]
                    masked = pr[0:qn, u % 3, 0:GROUP * nk]
                    if u == 0:
                        e.wait_ge(s_cb, 16)
                    e.wait_ge(s_s, u + 1)
                    if u >= 3:
                        e.wait_ge(s_t, u - 2)
                    e.tensor_tensor(masked, bank(u % 2)[0:qn, 0:GROUP * nk],
                                    cb[0:qn, B_M0:B_M1] if j == 0 else cb[0:qn, B_M1:B_END],
                                    ALU.add).then_inc(s_mask, 1)
                    e.wait_ge(s_mask, u + 1)
                    if u >= 4:
                        e.wait_ge(s_exp, u - 3)
                    e.tensor_reduce(NEGM[0:qn, u % 4, :],
                                    masked.rearrange("p (h k) -> p h k", h=GROUP), AX.X, ALU.max, negate=True).then_inc(s_max, 1)

                for j in range(NJ):
                    if j in FIRST_UNITS:
                        row_max(FIRST_UNITS[j])
                    e.wait_ge(s_vhi, j + 1)
                    e.tensor_tensor(v_hl[0:NK[j], LO, j, :], bank(4 + j % 2)[0:NK[j], :],
                                    f32(v_hl[0:NK[j], HI, j, :]), ALU.subtract).then_inc(s_vlo, 1)
                recip(0)
                recip(1)
                e.wait_ge(s_gwh, 1)
                e.tensor_tensor(gw_hl[:, GW_PARTS // 2:GW_PARTS], par[:, PR_GW:PR_END], f32(gw_hl[:, 0:GW_PARTS // 2]),
                                ALU.subtract).then_inc(s_gwl, 1)

                def pT_lo(u):
                    n, nk = GROUP * QN[units[u][1]], NK[units[u][1]]
                    e.wait_ge(s_phi, u + 1)
                    e.tensor_tensor(pT_hl[0:nk, u % 2, LO, 0:n], bank(2 + u % 2)[0:nk, 0:n],
                                    f32(pT_hl[0:nk, u % 2, HI, 0:n]), ALU.subtract).then_inc(s_plo, 1)

                def oT_lo(u):
                    g, j = units[u]
                    e.wait_ge(s_ohi, u + 1)
                    seg = slice(Q0[j], Q0[j] + QN[j])
                    e.tensor_tensor(oT_hl[:, LO, :, seg],
                                    bank(4 + u % 2)[:, 0:GROUP * QN[j]].rearrange("p (h q) -> p h q", h=GROUP),
                                    f32(oT_hl[:, HI, :, seg]), ALU.subtract).then_inc(s_olo, 1)

                def add(n):
                    e.wait_ge(s_y, n + 1)
                    if n >= NT:
                        e.wait_ge(s_add, n - NT + 1)
                    e.tensor_tensor(x[:, n % NT, :], bank(7)[:, 0:D], x[:, n % NT, :], ALU.add).then_inc(s_add, 1)

                for i in range(STEPS):
                    if len(FIRST_UNITS) <= i < NU:
                        row_max(i)
                    if 2 <= i - 1 < NU:
                        recip(i - 1)
                    if 0 <= i - LAG_P < NU:
                        pT_lo(i - LAG_P)
                    if i in y_tile:
                        add(y_tile[i])
                        if y_tile[i] >= (KV - 1) * NT:
                            early(phase, "stats", e, y_tile[i] % NT)
                    if 0 <= i - LAG_F < NU:
                        oT_lo(i - LAG_F)
                    for step, stage in ((NU, "veps0"), (NU + 1, "norm0"), (NU + 2, "lo0"), (NU + 3, "logits_copy0"),
                                        (NU + 4, "split0")):
                        if i == step:
                            early(phase, stage, e)

            def pool(e):
                e.memset(minus_half[:, :], -0.5).then_inc(s_init, 1)
                ln["rstd"](e, 0)
                ln["rstd"](e, 1)
                for n in range(5):
                    w_lo(e, n)
                for i in range(NU + 1):
                    if i >= 1:
                        u = i - 1
                        qn, nk = QN[units[u][1]], NK[units[u][1]]
                        e.wait_ge(s_rd, u + 1)
                        p3 = pr[0:qn, u % 3, 0:GROUP * nk].rearrange("p (h k) -> p h k", h=GROUP)
                        e.tensor_tensor(p3, p3, spread(RDEN[0:qn, u % 4, :], nk), ALU.mult).then_inc(s_nrm, 1)
                    if i in w_step:
                        w_lo(e, w_step[i])
                early(phase, "rstd0", e)

            def x_ready(e, t):
                e.wait_ge(s_add, (KV - 1) * NT + t + 1)

            def queries_done(e):
                e.wait_ge(s_q, KV * 2 * GROUP)
                e.wait_ge(s_wl, len(loads))

            def banks_free(e):
                queries_done(e)
                e.wait_ge(s_qt, KV * 2 * GROUP)
                e.wait_ge(s_exp, NU)

            phase.update(sync=sync, pe=pe, act=act, dve=dve, pool=pool, x_ready=x_ready, queries_done=queries_done,
                         xt_free=lambda e, h: queries_done(e), banks_free=banks_free, spare=6,
                         free=lambda e: e.wait_ge(s_add, KV * NT),
                         banks_free2=lambda e: e.wait_ge(s_olo, NU),
                         us_free=lambda e: (e.wait_ge(s_o, NU), e.wait_ge(s_y, (KV - 1) * NT)), kv_done=lambda e: e.wait_ge(s_o, NU))
            return phase

        w_hl = at("ffn_w_hl", [P, 2, F_END], F32R, A_V)
        NPIECE = len(F_CUTS) - 1
        s_fraw = [sem(f"ffn_raw{n}") for n in range(NPIECE)]
        s_fwh, s_fwl_dve, s_fwl_pool = sem("ffn_w_hi"), sem("ffn_w_lo_dve"), sem("ffn_w_lo_pool")
        F_LO_DVE, F_LO_POOL = (0, 1, 4, 6), (2, 3, 5, 7)
        f_raw = at("ffn_w_raw", [P, F_END], F32, A_W)
        assert A_V + 2 * F_END * 4 <= A_W and A_W + F_END * 4 <= A_Q

        F_EVENTS = dict(lg=2, lgt=2, lgr=2, lgc=2, m8=NT, ix=NT, ixf=2, hot=4, mt=1, mtT=1, gm=1, dg=1, nm=1, nmc=1, ex=SLOTS, sum=1,
                        rs=1, wt=1, wb=4, wbc=4, u=4, uhi=4, ulo=4, mk=4, mk0=2, mk1=4, um_dve=4, um_pool=12,
                        da=2, dd0=4, dd=2, dh=2, dl=2, y=2, add=4)
        F_EVENTS |= {n: 2 * HB for n in "a b d sil0 sil1 t0 t1 ch0 ch1 mix mxh mxl".split()} | dict(chh=4 * HB, chl=4 * HB)
        FS = {n: sem(f"ffn_{n}") for n in F_EVENTS}

        def ffn(tag, first, before):
            um_hl = at(f"{tag}_um", [P, 2, SLOTS, 2, 2, HALF], F32R, A_Q)
            wb = at(f"{tag}_wb", [P, SLOTS, T], F32, A_Q + 32768)
            mT = at(f"{tag}_mT", [P, 3, T], BF16, A_Q + 40960)
            hot = at(f"{tag}_hot", [P, SLOTS, NT, P], BF16, A_Q + 47104)
            U_CH = A_Q + 51200
            us_hl = at(f"{tag}_us", [P, 2, 2, 2, HALF], F32R, U_CH + 8192)
            assert U_CH + 24576 <= 229344
            ch_hl = at(f"{tag}_ch_hl", [P, 2, SLOTS, 2, HALF], F32R, A_W)
            mix_hl = at(f"{tag}_mix_hl", [P, 2, 2, HALF], F32R, A_W + 16384)
            sil = at(f"{tag}_sil", [P, SLOTS, HALF], F32, A_W + 24576)
            tt = at(f"{tag}_t", [P, SLOTS, HALF], F32, A_W + 28672)
            lgT = at(f"{tag}_lgT", [EXPERTS, HALF], F32, A_W + 30720)
            ch = at(f"{tag}_ch", [P, 2, SLOTS, HALF], F32, U_CH)
            mix = at(f"{tag}_mix", [P, 2, HALF], F32, U_CH + 8192)
            dd = at(f"{tag}_dd", [P, 3, HALF], F32, U_CH + 12288)
            d_hl = at(f"{tag}_d_hl", [P, 2, HALF], F32R, U_CH + 18432)
            lg = small[:, 0:64]
            m8 = small[:, 64:128].rearrange("p (t k) -> p t k", k=8)
            idx = small[:, 128:192].bitcast(U32)
            idxf = lg.rearrange("p (t k) -> p t k", k=8)
            MT, GM, DG, NM, SUM, RS = sm[:, 0:2], sm[0:2, 2:3], sm[0:2, 4:6], sm[:, 6:8], sm[:, 8:10], sm[:, 10:12]
            EX = sm[:, 16:32].rearrange("p (k t) -> p k t", k=2)
            WT = sm[:, 32:48].rearrange("p (k t) -> p k t", k=2)

            turn = 0 if first else 1
            N = 2 * HB

            def need(e, name, n):
                e.wait_ge(FS[name], turn * F_EVENTS[name] + n)

            ln = layer_norm(before["x_ready"], before["xt_free"], ((before["spare"], 0), (6, 7)),
                            lambda e, h: before["banks_free"](e) if h == 0 else before["free"](e))
            phase = {"next": {}}

            def blk(w, b, o, n=P):
                o += F_BLK + b * FB
                return w_hl[:, w, o:o + n]

            def upA(which, w, k):
                o = (F_UPA, F_GTA)[which] + k * P
                return w_hl[:, w, o:o + P]

            def piece(n):
                return slice(F_CUTS[n], F_CUTS[n + 1])

            def weights(e, pieces):
                for mine, s in ((F_LO_DVE, s_fwl_dve), (F_LO_POOL, s_fwl_pool)):
                    if set(mine) & set(pieces):
                        e.wait_ge(s, max(mine.index(n) + 1 for n in mine if n in pieces))

            def w_hi(e, n):
                e.wait_ge(s_fraw[n], 16)
                e.activation(w_hl[:, HI, piece(n)], f_raw[:, piece(n)], ACT.Copy).then_inc(s_fwh, 1)

            def w_lo(e, n):
                e.wait_ge(s_fwh, n + 1)
                e.tensor_tensor(w_hl[:, LO, piece(n)], f_raw[:, piece(n)], f32(w_hl[:, HI, piece(n)]),
                                ALU.subtract).then_inc(s_fwl_dve if n in F_LO_DVE else s_fwl_pool, 1)

            def half(h):
                return slice(HALF * h, HALF * h + HALF)

            def wb_bank(h, s):
                return 6 + s if h == 0 else 4 + s

            def sync(e):
                if not first:
                    return
                before["queries_done"](e)
                for n in range(NPIECE):
                    e.dma_start(f_raw[:, piece(n)], ins["ffn"][:, piece(n)]).then_inc(s_fraw[n], 16)

            def logits(e, h):
                ln["ready"](e, h)
                e.wait_ge(s_gwl, 1)
                for k in range(KB):
                    m = three(e, bank((1, 6)[h]),
                              lambda w: gw_hl[:, (w * KB + k) * EXPERTS:(w * KB + k) * EXPERTS + P],
                              lambda w: xT[:, w, k, half(h)], k == 0, k == KB - 1)
                m.then_inc(FS["lg"], 1)

            def logits_copy(e, h):
                need(e, "lg", h + 1)
                e.tensor_copy(lgT[:, :], bank((1, 6)[h])[0:EXPERTS, :]).then_inc(FS["lgt"], 1)

            def logits_tr(e, h):
                need(e, "lgt", h + 1)
                for i in range(HT):
                    m = e.transpose(bank((1, 6)[h])[:, i * 8:i * 8 + 8], lgT[:, i * P:(i + 1) * P],
                                    ident[0:EXPERTS, 0:EXPERTS])
                m.then_inc(FS["lgr"], 1)

            def top(e, h):
                seg = slice(32 * h, 32 * h + 32)
                need(e, "lgr", h + 1)
                e.tensor_copy(lg[:, seg], bank((1, 6)[h])[:, 0:32]).then_inc(FS["lgc"], 1)
                need(e, "lgc", h + 1)
                tiles = range(HT * h, HT * h + HT)
                for t in tiles:
                    e.max(m8[:, t, :], lg[:, 8 * t:8 * t + 8]).then_inc(FS["m8"], 1)
                for t in tiles:
                    need(e, "m8", t + 1)
                    e.max_index(idx[:, 8 * t:8 * t + 8], m8[:, t, :], lg[:, 8 * t:8 * t + 8]).then_inc(FS["ix"], 1)
                if h:
                    e.tensor_reduce(MT, m8[:, :, 0:2].rearrange("p t k -> p k t"), AX.X, ALU.max).then_inc(FS["mt"], 1)
                need(e, "ix", HT * (h + 1))
                e.tensor_copy(lg[:, seg], idx[:, seg]).then_inc(FS["ixf"], 1)

            def lora_a(e, h, parts=(0, 1)):
                if h == 0:
                    weights(e, [0])
                    before["banks_free2"](e)
                else:
                    need(e, "mk0", 1)
                    need(e, "mk1", 2)
                for which in parts:
                    for k in range(KB):
                        m = three(e, bank(4 + which), lambda w: upA(which, w, k),
                                  lambda w: xT[:, w, k, half(h)], k == 0, k == KB - 1)
                    m.then_inc(FS["u"], 1)

            def masks(e, h):
                need(e, "ulo", 2 * h + 2)
                need(e, "hot", 2 * h + 2)
                for s in range(SLOTS):
                    for t in range(HT):
                        m = e.matmul(bank(4 + s)[:, t * P:(t + 1) * P], hot[:, s, HT * h + t, :], identb,
                                     start=True, stop=True)
                    m.then_inc(FS["mk"], 1)

            def base_x(e, i):
                h, b = divmod(i, HB)
                weights(e, [1 + b])
                if i == 0:
                    before["banks_free2"](e)
                if i == 1:
                    need(e, "lgc", 1)
                if i >= 2:
                    need(e, "t1", i - 1)
                for which in range(2):
                    for k in range(KB):
                        three(e, bank(2 * which + i % 2), lambda w: blk(w, b, (FB_UP, FB_GT)[which] + k * P),
                              lambda w: xT[:, w, k, half(h)], k == 0, k == KB - 1)

            def base_lora(e, i):
                h, b = divmod(i, HB)
                if i == 0:
                    need(e, "um_dve", 4)
                if i == HB:
                    need(e, "um_pool", 8)
                for which in range(2):
                    m = three(e, bank(2 * which + i % 2), lambda w: blk(w, b, (FB_UPB, FB_GTB)[which]),
                              lambda w: um_hl[:, h, 0, which, w, :], False, True, skip_group_check=True)
                m.then_inc(FS["a"], 1)

            def pe(e):
                def second(i):
                    h, b = divmod(i, HB)
                    if b == 0:
                        need(e, "um_pool", 12 if h else 4)
                    need(e, "t0", i + 1)
                    for which in range(2):
                        m = three(e, bank(2 * which + i % 2), lambda w: blk(w, b, (FB_UPB, FB_GTB)[which]),
                                  lambda w: um_hl[:, h, 1, which, w, :], False, True, skip_group_check=True)
                    m.then_inc(FS["b"], 1)

                ln["tr"](e, 1)
                masks(e, 0)
                logits(e, 1)
                base_x(e, 1)
                logits_tr(e, 1)
                base_lora(e, 0)
                need(e, "mt", 1)
                e.transpose(bank(7)[0:2, 0:P], MT, ident).then_inc(FS["mtT"], 1)
                base_lora(e, 1)
                lora_a(e, 1, (0,))
                need(e, "dg", 1)
                e.matmul(bank(7)[:, P:P + 2], ones[0:2, :], DG, start=True, stop=True).then_inc(FS["nm"], 1)
                lora_a(e, 1, (1,))
                need(e, "ex", SLOTS)
                e.matmul(bank(7)[:, P + 2:P + 4], ones, SUM, start=True, stop=True).then_inc(FS["sum"], 1)
                masks(e, 1)
                need(e, "wt", 1)
                for h in range(2):
                    if h:
                        need(e, "mk0", 2)
                        need(e, "mk1", 4)
                    for s in range(SLOTS):
                        for i in range(HT):
                            t = HT * h + i
                            m = e.matmul(bank(wb_bank(h, s))[:, i * P:(i + 1) * P],
                                         WT[:, s, t:t + 1].broadcast_to([P, P]), ident, start=True, stop=True)
                        m.then_inc(FS["wb"], 1)
                    if h == 0:
                        second(0)

                def down(i):
                    h, b = divmod(i, HB)
                    if i == 0:
                        need(e, "wbc", 4)
                    if h == 1 and b == 0:
                        need(e, "dd0", 2)
                    need(e, "chl", 2 * (i + 1))
                    for s in range(SLOTS):
                        m = three(e, bank(6 + s), lambda w: blk(w, b, FB_DA, ER),
                                  lambda w: ch_hl[:, i % 2, s, w, :], b == 0, b == HB - 1)
                    if b == HB - 1:
                        m.then_inc(FS["da"], 1)
                    if h == 1 and b == 0:
                        need(e, "add", 2)
                    need(e, "mxl", i + 1)
                    for t in range(HT):
                        m = three(e, bank(4 + t // 2)[:, (t % 2) * D:(t % 2 + 1) * D],
                                  lambda w: mix_hl[:, i % 2, w, t * P:(t + 1) * P],
                                  lambda w: blk(w, b, FB_DN, D),
                                  b == 0 and t % 2 == 0, False, skip_group_check=True)
                    m.then_inc(FS["d"], 1)

                def lora_down(h):
                    weights(e, [NPIECE - 1])
                    need(e, "dl", h + 1)
                    for t in range(HT):
                        m = three(e, bank(4 + t // 2)[:, (t % 2) * D:(t % 2 + 1) * D],
                                  lambda w: d_hl[:, w, t * P:(t + 1) * P], lambda w: w_hl[:, w, F_DB:F_DB + D],
                                  False, True, skip_group_check=True)
                    m.then_inc(FS["y"], 1)

                for i in range(N + 2):
                    if 2 <= i < N:
                        base_x(e, i)
                        base_lora(e, i)
                    if i == N:
                        early(phase, "tr0", e)
                    if 2 <= i <= N:
                        second(i - 1)
                    if i == HB + 2:
                        lora_down(0)
                    if i >= 2:
                        down(i - 2)
                early(phase, "in_proj0", e)
                lora_down(1)

            def act(e):
                def split(*pieces):
                    if first:
                        for n in pieces:
                            w_hi(e, n)

                def a_hi(h, parts=(0, 1)):
                    for which in parts:
                        need(e, "u", 2 * h + which + 1)
                        e.activation(us_hl[:, h, which, HI, :], bank(4 + which), ACT.Copy,
                                     scale=ALPHA).then_inc(FS["uhi"], 1)

                def mask0(h):
                    need(e, "mk", 2 * h + 1)
                    e.activation(mT[:, 0, half(h)], bank(4), ACT.Copy).then_inc(FS["mk0"], 1)

                if first:
                    before["kv_done"](e)
                split(0, 1, 2)
                before["us_free"](e)
                a_hi(0)
                ln["hi"](e, 1)
                before["free"](e)
                mask0(0)
                split(3, 4, 5, 6, 7)
                a_hi(1, (0,))
                need(e, "nmc", 1)
                for s in range(SLOTS):
                    e.activation(EX[:, s, :], m8[:, :, s], ACT.Exp, bias=NM[:, s:s + 1],
                                 accum_out=SUM[:, s:s + 1]).then_inc(FS["ex"], 1)

                def silu(i, s):
                    need(e, "ab"[s], i + 1)
                    if i >= 1:
                        need(e, f"t{s}", i)
                    e.activation(sil[:, s, :], bank(i % 2), ACT.Silu).then_inc(FS[f"sil{s}"], 1)

                a_hi(1, (1,))
                mask0(1)
                if first:
                    weights(e, range(NPIECE))
                for h in range(2):
                    silu(0, h)
                    for s in range(SLOTS):
                        need(e, "wb", 2 * h + s + 1)
                        e.activation(wb[:, s, half(h)], bank(wb_bank(h, s)), ACT.Copy).then_inc(FS["wbc"], 1)

                def hi_parts(i):
                    if i >= 2:
                        need(e, "d", i - 1)
                    for s in range(SLOTS):
                        need(e, f"ch{s}", i + 1)
                        e.activation(ch_hl[:, i % 2, s, HI, :], ch[:, i % 2, s, :], ACT.Copy).then_inc(FS["chh"], 1)
                    need(e, "mix", i + 1)
                    e.activation(mix_hl[:, i % 2, HI, :], mix[:, i % 2, :], ACT.Copy).then_inc(FS["mxh"], 1)

                def lora_hi(h):
                    need(e, "dd", h + 1)
                    if h:
                        need(e, "y", h)
                    e.activation(d_hl[:, HI, :], dd[:, 2, :], ACT.Copy).then_inc(FS["dh"], 1)

                for i in range(N + 1):
                    if i == HB + 2:
                        lora_hi(0)
                    if 1 <= i < N:
                        silu(i, 0)
                    if i >= 2:
                        silu(i - 1, 1)
                    if i >= 1:
                        hi_parts(i - 1)
                    if i == N - 1:
                        early(phase, "w_hi0", e)
                early(phase, "hi0", e)
                lora_hi(1)

            def dve(e):
                def split(*pieces):
                    if first:
                        for n in pieces:
                            w_lo(e, n)

                def one_hot(h):
                    need(e, "ixf", h + 1)
                    seg = slice(HT * h, HT * h + HT)
                    for s in range(SLOTS):
                        e.tensor_tensor(hot[:, s, seg, :], repeat(cb[:, B_ECOL:B_ECOL + P], HT),
                                        spread(idxf[:, seg, s], P), ALU.is_equal).then_inc(FS["hot"], 1)

                def a_lo(h):
                    for which in range(2):
                        need(e, "uhi", 2 * h + which + 1)
                        e.scalar_tensor_tensor(out=us_hl[:, h, which, LO, :], in0=bank(4 + which), scalar=ALPHA,
                                               in1=f32(us_hl[:, h, which, HI, :]), op0=ALU.mult,
                                               op1=ALU.subtract).then_inc(FS["ulo"], 1)

                def mask1(h):
                    need(e, "mk0", h + 1)
                    need(e, "mk", 2 * h + 2)
                    e.tensor_copy(mT[:, 1, half(h)], bank(5)).then_inc(FS["mk1"], 1)
                    e.tensor_tensor(mT[:, 2, half(h)], bank(5), mT[:, 0, half(h)], ALU.subtract).then_inc(FS["mk1"], 1)

                def gated(i, s):
                    need(e, f"sil{s}", i + 1)
                    if i >= 1:
                        need(e, f"ch{s}", i)
                    e.tensor_tensor(tt[:, s, :], bank(2 + i % 2), sil[:, s, :], ALU.mult).then_inc(FS[f"t{s}"], 1)

                ln["veps"](e, 1)
                top(e, 0)
                ln["norm"](e, 1)
                before["us_free"](e)
                a_lo(0)
                before["free"](e)
                one_hot(0)
                ln["lo"](e, 1)
                mask1(0)
                logits_copy(e, 1)
                for which in range(2):
                    for w in (HI, LO):
                        e.tensor_tensor(um_hl[:, 0, 0, which, w, :], f32(us_hl[:, 0, which, w, :]),
                                        mT[:, 0, half(0)], ALU.mult).then_inc(FS["um_dve"], 1)
                top(e, 1)
                need(e, "mtT", 1)
                e.tensor_reduce(GM, bank(7)[0:2, 0:P], AX.X, ALU.max, negate=True).then_inc(FS["gm"], 1)
                need(e, "gm", 1)
                e.tensor_scalar(DG, ident[0:2, 0:2], GM, None, ALU.mult).then_inc(FS["dg"], 1)
                one_hot(1)
                need(e, "nm", 1)
                e.tensor_copy(NM, bank(7)[:, P:P + 2]).then_inc(FS["nmc"], 1)
                a_lo(1)
                need(e, "sum", 1)
                e.reciprocal(RS, bank(7)[:, P + 2:P + 4]).then_inc(FS["rs"], 1)
                need(e, "rs", 1)
                e.tensor_tensor(WT, EX, spread(RS, NT), ALU.mult).then_inc(FS["wt"], 1)
                split(4, 6)
                mask1(1)
                gated(0, 0)
                gated(0, 1)

                def slot(i, s):
                    h = i // HB
                    if i:
                        gated(i, s)
                    need(e, f"t{s}", i + 1)
                    if i % HB == 0 and s == 0:
                        need(e, "wbc", 2 * h + 2)
                    if i >= 2:
                        need(e, "chl", 2 * (i - 1))
                        need(e, "mix", i - 1)
                    e.tensor_tensor(ch[:, i % 2, s, :], tt[:, s, :], wb[:, s, half(h)], ALU.mult).then_inc(FS[f"ch{s}"], 1)

                def lo_parts(i):
                    for s in range(SLOTS):
                        need(e, "chh", 2 * i + s + 1)
                        e.tensor_tensor(ch_hl[:, i % 2, s, LO, :], ch[:, i % 2, s, :], f32(ch_hl[:, i % 2, s, HI, :]),
                                        ALU.subtract).then_inc(FS["chl"], 1)
                    need(e, "mxh", i + 1)
                    e.tensor_tensor(mix_hl[:, i % 2, LO, :], mix[:, i % 2, :], f32(mix_hl[:, i % 2, HI, :]),
                                    ALU.subtract).then_inc(FS["mxl"], 1)

                def lora_mask(h):
                    need(e, "da", h + 1)
                    need(e, "um_pool", 12)
                    if h:
                        need(e, "dl", h)
                    for s in range(SLOTS):
                        e.scalar_tensor_tensor(out=dd[:, s, :], in0=bank(6 + s), scalar=ALPHA, in1=mT[:, s, half(h)],
                                               op0=ALU.mult, op1=ALU.mult).then_inc(FS["dd0"], 1)
                    need(e, "dd0", 2 * (h + 1))
                    e.tensor_tensor(dd[:, 2, :], dd[:, 0, :], dd[:, 1, :], ALU.add).then_inc(FS["dd"], 1)
                    need(e, "dh", h + 1)
                    e.tensor_tensor(d_hl[:, LO, :], dd[:, 2, :], f32(d_hl[:, HI, :]), ALU.subtract).then_inc(FS["dl"], 1)

                def add(h):
                    need(e, "y", h + 1)
                    for b in range(2):
                        t = HT * h + 2 * b
                        e.tensor_tensor(x[:, t:t + 2, :], bank(4 + b).rearrange("p (t n) -> p t n", t=2),
                                        x[:, t:t + 2, :], ALU.add).then_inc(FS["add"], 1)

                for i in range(N + 1):
                    if i == HB + 2:
                        lora_mask(0)
                    if i < N:
                        slot(i, 0)
                    if i == HB + 2:
                        add(0)
                        early(phase, "stats", e, *range(HT))
                        early(phase, "veps0", e)
                    if i == HB + 4:
                        early(phase, "norm0", e)
                    if i >= 1:
                        slot(i - 1, 1)
                        lo_parts(i - 1)
                    if i == N - 1:
                        early(phase, "w_lo0", e)
                early(phase, "lo0", e)
                lora_mask(1)
                add(1)

            def pool(e):
                def split(*pieces):
                    if first:
                        for n in pieces:
                            w_lo(e, n)

                def masked(h, s):
                    for which in range(2):
                        for w in (HI, LO):
                            e.tensor_tensor(um_hl[:, h, s, which, w, :], f32(us_hl[:, h, which, w, :]),
                                            mT[:, (0, 2)[s], half(h)], ALU.mult).then_inc(FS["um_pool"], 1)

                ln["rstd"](e, 1)
                split(2, 3)
                need(e, "ulo", 2)
                need(e, "mk1", 2)
                masked(0, 1)
                split(5, 7)
                need(e, "um_dve", 4)
                need(e, "um_pool", 4)
                for i in range(N):
                    if i == HB + 3:
                        early(phase, "rstd0", e)
                    if i in (1, 2):
                        need(e, "ulo", 4)
                        need(e, "mk1", 4)
                        masked(1, i - 1)
                    for s in range(SLOTS):
                        need(e, f"ch{s}", i + 1)
                    if i >= 2:
                        need(e, "mxl", i - 1)
                    e.tensor_tensor(mix[:, i % 2, :], ch[:, i % 2, 0, :], ch[:, i % 2, 1, :], ALU.add).then_inc(FS["mix"], 1)

            def split0(e):
                if first:
                    for n in (0, 1):
                        w_lo(e, n)

            phase.update(early_stages(ln))
            phase.update(sync=sync, pe=pe, act=act, dve=dve, pool=pool, split0=split0,
                         logits0=lambda e: logits(e, 0), logits_copy0=lambda e: logits_copy(e, 0),
                         logits_tr0=lambda e: logits_tr(e, 0),
                         lora_a0=lambda e: lora_a(e, 0), base_x0=lambda e: base_x(e, 0),
                         x_ready=lambda e, t: need(e, "add", t // 2 + 1),
                         xt_free=lambda e, h: need(e, "a", HB * (h + 1)),
                         free=lambda e: need(e, "add", 4),
                         banks_free=lambda e: need(e, "t1", N - 1),
                         um0_done=lambda e: need(e, "b", HB), loop_done=lambda e: need(e, "d", N))
            return phase

        def mixer(before):
            wm_hl = at("ssd_w_hl", [P, 2, M_END], F32R, A_W)
            w0_hl = at("ssd_w0_hl", [P, 2, M_CUTS[1]], F32R, A_Q + 47104)
            m_raw = at("ssd_w_raw", [P, M_END], F32, A_Q)
            GAP = A_V + 2 * F_END * 4
            XR = T + CONV - 1
            xr = [at(f"conv_in{n}", [P, XR], F32, o) for n, o in enumerate((GAP, A_Q + 4 * M_END))]
            sd = at("ssd_small", [P, 13 * 32], F32, GAP + 4128)
            assert GAP + 4128 + 13 * 128 <= A_W
            Z0 = A_Q + 4 * M_END + 4128
            zs = at("silu_z", [P, NH, T], F32, Z0)
            xs = at("xs", [P, NH, T], F32, Z0 + 16384)
            xsD = at("xs_D", [P, NH, T], F32, Z0 + 32768)
            bcT = at("bcT", [P, 2, T], F32, Z0 + 49152)
            assert Z0 + 57344 <= 229344
            V, AV, E1, U1, L1, D1, Z1, N1, R1, SP, DT, AA, RL = (sd[:, 32 * i:32 * i + 32] for i in range(13))
            AAH, AAL = V, AV
            AN, VE, RI = sm[:, 0:4], sm[:, 8:16], sm[:, 16:24]
            slots = ([A_W + 2048 * i for i in range(5)] + [A_W + 4 * M_END + 2048 * i for i in range(5)]
                     + [A_Q + 2048 * i for i in range(9)] + [A_W + 8 * M_END + 2048 * i for i in range(2)]
                     + [GAP, GAP + 2048])

            def pair(name, dt=F32):
                return [at(f"{name}{n}", [P, NH, P], dt, slots.pop(0))[:, :, :] for n in range(2)]

            ar_hi, Lm, ecs, xd, xdd, wt = (pair(n, F32R if n == "ar_hi" else F32) for n in ("ar_hi", "decay", "expcs", "x_dt", "x_dt_decay", "w_mix"))
            ce, st, gy, g2 = (pair(n) for n in ("c_exp", "state", "gated", "gated_sq"))
            st_t = at("state_decayed", [P, NH, P], F32, slots.pop(0))[:, :, :]
            g_hi, g_lo = (at(n, [P, NH, P], F32R, slots.pop(0))[:, :, :] for n in ("g_hi", "g_lo"))
            btok = at("b_tok", [P, 2, STATE], F32, Z0 + 57344)
            ar_lo = at("ar_lo", [P, NH, P], F32R, Z0 + 57856)[:, :, :]
            after_r, ones_r = (at(n, [P, P], F32R, Z0 + o)[:, :] for n, o in (("after_r", 59904), ("ones_r", 60416)))
            cbm = at("c_b_masked", [P, P], F32, Z0 + 60928)[:, :]
            assert Z0 + 61440 <= 229344 and not slots
            CONVS = [0] + list(range(2, CB))
            dst = lambda b: cb_pre[:, :] if b == 0 else xs[:, b - 2, :]
            cb_pre = at("conv_cb", [P, T], F32, Z0 + 4096 * (NH - 1))

            names = ("xda cbm gs arl cst raw wh wl0 wl1 wl2 wl3 nw pad ip ipx cv sl xd dt dt_dve dt_act ar de L G xt X xdd wt ce Y St st1 st y g ghi glo g2 ss "
                     "ve ri O fin bt").split()
            S = {n: sem(f"ssd_{n}") for n in names}
            ln = layer_norm(before["x_ready"], before["xt_free"], ((0, 2), (1, 3)),
                            lambda e, h: before["banks_free"](e) if h == 0 else before["free"](e))
            phase = {"next": {}}
            upto = cf[:, C_UPTO:C_UPTO + P]
            after = cf[:, C_AFTER:C_AFTER + P]
            DT_DONE = 16
            NB = CB + NH
            order = [(0, 0), (1, 0), (1, 1), (0, 1)] + [(b, h) for b in (2, 3, 6, 4, 7, 5, 8, 9) for h in range(2)]
            IN_BANK = [0, 2, 1, 3] + [4 + n % 3 for n in range(4, 2 * NB)]
            after_copy = {}
            for n in range(2 * NB):
                former = [m for m in range(n) if IN_BANK[m] == IN_BANK[n]]
                after_copy[n] = former[-1] + 1 if former else 0
            PIECE_OF = [0, 0, 1, 1, 1, 1, 2, 2, 2, 2]

            def piece(n):
                return slice(M_CUTS[n], M_CUTS[n + 1])

            def w_part(n, which):
                return w0_hl[:, which, :] if n == 0 else wm_hl[:, which, piece(n)]

            def w_hi(e, n):
                e.wait_ge(S["raw"], 16 * 4)
                e.activation(w_part(n, HI), m_raw[:, piece(n)], ACT.Copy).then_inc(S["wh"], 1)

            def w_lo(e, n):
                e.wait_ge(S["wh"], n + 1)
                e.tensor_tensor(w_part(n, LO), m_raw[:, piece(n)], f32(w_part(n, HI)),
                                ALU.subtract).then_inc(S[f"wl{n}"], 1)

            def in_proj(e, n):
                b, h = order[n]
                w_of = w0_hl if b < 2 else wm_hl
                e.wait_ge(S[f"wl{PIECE_OF[b]}"], 1)
                e.wait_ge(S["ipx"], after_copy[n])
                for k in range(KB):
                    o = M_IN + (b * KB + k) * P
                    m = three(e, bank(IN_BANK[n]), lambda w: w_of[:, w, o:o + P], lambda w: xT[:, w, k, half(h)],
                              k == 0, k == KB - 1)
                m.then_inc(S["ip"], 1)

            def in_proj0(e):
                ln["ready"](e, 0)
                for n in range(2):
                    in_proj(e, n)

            def half(h):
                return slice(HALF * h, HALF * h + HALF)

            def tile(c):
                return slice(P * c, P * c + P)

            def sync(e):
                before["um0_done"](e)
                for n in range(4):
                    e.dma_start(m_raw[:, piece(n)], ins["ssd"][:, piece(n)]).then_inc(S["raw"], 16)

            def pe(e):
                ln["tr"](e, 1)
                ln["ready"](e, 1)
                in_proj(e, 2)
                in_proj(e, 3)
                before["free"](e)
                e.wait_ge(S["ipx"], 3)
                for t in range(NT):
                    m = e.transpose(bank(7)[:, t * NH:(t + 1) * NH],
                                    xr[1][0:NH, CONV - 1 + t * P:CONV - 1 + (t + 1) * P], ident[0:NH, 0:NH])
                m.then_inc(S["dt"], 1)
                for n in range(4, 2 * NB):
                    in_proj(e, n)

                def decays(c):
                    e.wait_ge(S["ar"], c + 1)
                    e.wait_ge(S["arl"], c + 1)
                    if c == 0:
                        e.wait_ge(S["ipx"], 4)
                        e.wait_ge(S["cst"], 1)
                    else:
                        e.wait_ge(S["L"], 2 * c)
                    rhs = [a.rearrange("p h l -> p (h l)") for a in (ar_hi[c % 2], ar_lo)]
                    for w in (HI, LO):
                        e.matmul(bank(0), after_r, rhs[w], start=w == HI, stop=w == LO)
                    for w in (HI, LO):
                        m = e.matmul(bank(1), ones_r, rhs[w], start=w == HI, stop=w == LO)
                    m.then_inc(S["de"], 1)
                    if c == 0:
                        e.wait_ge(S["sl"], 2)
                    else:
                        e.wait_ge(S["cbm"], c)
                        e.wait_ge(S["bt"], c)
                    e.matmul(bank(2)[:, 0:P], bcT[0:STATE, 0, tile(c)], bcT[0:STATE, 1, tile(c)], start=True, stop=True)
                    e.transpose(bank(2)[:, P:P + STATE], bcT[0:STATE, 0, tile(c)], ident[0:STATE, 0:STATE]).then_inc(S["G"], 1)
                    if c == 0:
                        e.wait_ge(S["sl"], CB)
                    else:
                        e.wait_ge(S["X"], c)
                    for h in range(NH):
                        m = e.transpose(bank(3)[:, tile(h)], xs[:, h, tile(c)], ident)
                    m.then_inc(S["xt"], 1)

                def outputs(c):
                    e.wait_ge(S["ce"], c + 1)
                    if c:
                        e.wait_ge(S["st"], c)
                        e.wait_ge(S["y"], c)
                    e.wait_ge(S["X"], c + 1)
                    for h in range(NH):
                        m = e.matmul(bank(4)[:, tile(h)], xd[c % 2][:, h, :], wt[c % 2][:, h, :], start=True, stop=c == 0)
                        if c:
                            m = e.matmul(bank(4)[:, tile(h)], st[c % 2][0:STATE, h, :], ce[c % 2][0:STATE, h, :],
                                         start=False, stop=True)
                    m.then_inc(S["Y"], 1)
                    if c < NT - 1:
                        e.wait_ge(S["xdd"], c + 1)
                        e.wait_ge(S["bt"], c + 1)
                        e.matmul(bank(5)[0:STATE, :], btok[:, c % 2, :], xdd[c % 2].rearrange("p h l -> p (h l)"),
                                 start=True, stop=True).then_inc(S["St"], 1)

                def project(c):
                    if c == 0:
                        e.wait_ge(S["wl3"], 1)
                    if c >= 2:
                        e.wait_ge(S["fin"], c - 1)
                    if c == 1:
                        e.wait_ge(S["dt_dve"], 1)
                    e.wait_ge(S["gs"], 2 * c + 2)
                    e.matmul(bank(6 + c % 2)[:, D:D + 1], g2[c % 2][:, 0, :], ones[:, 0:1], start=True,
                             stop=True).then_inc(S["ss"], 1)
                    e.wait_ge(S["glo"], c + 1)
                    for h in range(NH):
                        o = M_OUT + h * D
                        m = three(e, bank(6 + c % 2)[:, 0:D], lambda w: (g_hi, g_lo)[w][:, h, :],
                                  lambda w: wm_hl[:, w, o:o + D], h == 0, h == NH - 1)
                    m.then_inc(S["O"], 1)

                for i in range(NT + 3):
                    if i < NT:
                        decays(i)
                    if i >= 3:
                        project(i - 3)
                    if i == NT + 1:
                        early(phase, "tr0", e)
                    if 1 <= i <= NT:
                        outputs(i - 1)
                for stage in ("logits0", "lora_a0", "logits_tr0", "base_x0"):
                    early(phase, stage, e)

            def act(e):
                before["loop_done"](e)
                w_hi(e, 1)
                e.activation(after_r, after, ACT.Copy)
                e.activation(ones_r, ones, ACT.Copy).then_inc(S["cst"], 1)
                ln["hi"](e, 1)
                w_hi(e, 2)

                def conv_in(n):
                    b, h = order[n]
                    e.wait_ge(S["ip"], n + 1)
                    if h == 0 and b >= 2:
                        if b == 3:
                            e.wait_ge(S["dt"], 1)
                        else:
                            e.wait_ge(S["cv"], CONV * (CONVS.index(b - 2) + 1))
                    e.activation(xr[b % 2][:, CONV - 1 + HALF * h:CONV - 1 + HALF * h + HALF], bank(IN_BANK[n]),
                                 ACT.Copy).then_inc(S["ipx"], 1)

                def silu_z(n):
                    b, h = order[n]
                    e.wait_ge(S["ip"], n + 1)
                    e.wait_ge(S["sl"], 2)
                    e.activation(zs[:, b - CB, half(h)], bank(IN_BANK[n]), ACT.Silu).then_inc(S["ipx"], 1)

                def silu(b):
                    e.wait_ge(S["cv"], CONV * (CONVS.index(b) + 1))
                    if b == 0:
                        for n, rows in enumerate((slice(STATE, P), slice(0, STATE))):
                            e.activation(bcT[0:STATE, n, :], cb_pre[rows, :], ACT.Silu).then_inc(S["sl"], 1)
                        return
                    e.activation(dst(b), dst(b), ACT.Silu).then_inc(S["sl"], 1)

                for n in range(4):
                    conv_in(n)
                e.activation(AN, par[:, PR_AL:PR_AL + NH], ACT.Exp).then_inc(S["dt_act"], 1)
                e.wait_ge(S["dt_dve"], 2)
                e.activation(E1, AV, ACT.Exp, scale=-1.0).then_inc(S["dt_act"], 1)
                e.wait_ge(S["nw"], NH)
                w_hi(e, 3)
                for n in range(4, 8):
                    conv_in(n)
                e.wait_ge(S["dt_dve"], 4)
                e.activation(L1, U1, ACT.Ln).then_inc(S["dt_act"], 1)
                silu(0)
                for n in range(8, 2 * NB, 2):
                    b = order[n][0]
                    take = silu_z if b >= CB else conv_in
                    take(n)
                    take(n + 1)
                    if b < CB:
                        silu(b - 2)
                for b in (CB - 2, CB - 1):
                    silu(b)

                for i in range(NT + 2):
                    c = i
                    if c < NT:
                        e.wait_ge(S["de"], c + 1)
                        if c >= 2:
                            e.wait_ge(S["xdd"], c - 1)
                            e.wait_ge(S["ce"], c - 1)
                            e.wait_ge(S["st1"], c - 2)
                        e.activation(Lm[c % 2].rearrange("p h l -> p (h l)"), bank(0), ACT.Exp).then_inc(S["L"], 1)
                        e.activation(ecs[c % 2][0:STATE].rearrange("p h l -> p (h l)"), bank(1)[0:STATE, :],
                                     ACT.Exp).then_inc(S["L"], 1)
                        e.wait_ge(S["G"], c + 1)
                        if c >= 2:
                            e.wait_ge(S["St"], c - 1)
                        e.activation(btok[:, c % 2, :], bank(2)[:, P:P + STATE], ACT.Copy).then_inc(S["bt"], 1)
                        e.wait_ge(S["xt"], c + 1)
                        if c >= 2:
                            e.wait_ge(S["Y"], c - 1)
                        if c == 0:
                            e.wait_ge(S["dt_dve"], DT_DONE)
                        for h in range(NH):
                            m = e.activation(xd[c % 2][:, h, :], bank(3)[:, tile(h)], ACT.Copy,
                                             scale=DT[:, c * NH + h:c * NH + h + 1])
                        m.then_inc(S["X"], 1)
                    if c == 0:
                        e.wait_ge(S["sl"], CB)
                        e.activation(xsD[:, NH - 1, :], xs[:, NH - 1, :], ACT.Copy,
                                     scale=par[:, PR_D + NH - 1:PR_D + NH]).then_inc(S["xda"], 1)
                    if i >= 2:
                        c = i - 2
                        e.wait_ge(S["g"], c + 1)
                        if c:
                            e.wait_ge(S["O"], c)
                        e.activation(g_hi, gy[c % 2], ACT.Copy).then_inc(S["ghi"], 1)
                        if c >= 2:
                            e.wait_ge(S["ss"], c - 1)
                        e.activation(g2[c % 2], gy[c % 2], ACT.Square).then_inc(S["g2"], 1)
                early(phase, "hi0", e)

            def dve(e):
                ln["stats"](e, *range(HT, NT))
                ln["veps"](e, 1)
                w_lo(e, 1)
                ln["norm"](e, 1)
                ln["lo"](e, 1)
                w_lo(e, 2)

                def conv(b):
                    k0 = CONV * CONVS.index(b)
                    tap = lambda k: par[:, PR_CW + CONV * b + k:PR_CW + CONV * b + k + 1]
                    e.wait_ge(S["ipx"], order.index((b, 1)) + 1)
                    e.tensor_scalar(dst(b), xr[b % 2][:, CONV - 1:XR], tap(CONV - 1),
                                    par[:, PR_CB + b:PR_CB + b + 1], ALU.mult, ALU.add).then_inc(S["cv"], 1)
                    for k in range(CONV - 1):
                        e.wait_ge(S["cv"], k0 + k + 1)
                        e.scalar_tensor_tensor(out=dst(b), in0=xr[b % 2][:, k:k + T], scalar=tap(k), in1=dst(b),
                                               op0=ALU.mult, op1=ALU.add).then_inc(S["cv"], 1)

                e.wait_ge(S["pad"], 1)
                t3 = lambda a: a.rearrange("p (t h) -> p t h", h=NH)
                done = [0]

                def step(i):
                    i.then_inc(S["dt_dve"], 1)
                    done[0] += 1
                    e.wait_ge(S["dt_dve"], done[0])

                e.wait_ge(S["dt"], 1)
                step(e.tensor_tensor(t3(V), t3(bank(7)[:, 0:NT * NH]), repeat(par[:, PR_DTB:PR_DTB + NH], NT), ALU.add))
                step(e.scalar_tensor_tensor(out=AV, in0=V, scalar=-1.0, in1=V, op0=ALU.mult, op1=ALU.max))
                step(e.tensor_scalar(RL, V, 0.0, None, ALU.max))
                conv(0)
                e.wait_ge(S["dt_act"], 2)
                step(e.tensor_scalar(U1, E1, 1.0, None, ALU.add))
                step(e.tensor_scalar(D1, U1, -1.0, None, ALU.add))
                step(e.tensor_scalar(Z1, D1, 0.0, None, ALU.is_equal))
                step(e.tensor_tensor(N1, D1, Z1, ALU.add))
                step(e.reciprocal(R1, N1))
                step(e.tensor_tensor(SP, R1, E1, ALU.mult))
                step(e.tensor_scalar(AN, AN, -1.0, None, ALU.mult))
                conv(2)
                e.wait_ge(S["dt_act"], 3)
                step(e.tensor_tensor(N1, L1, Z1, ALU.add))
                step(e.tensor_tensor(SP, N1, SP, ALU.mult))
                step(e.tensor_tensor(DT, SP, RL, ALU.add))
                step(e.tensor_tensor(t3(AA), t3(DT), repeat(AN, NT), ALU.mult))
                step(e.tensor_copy(AAH.bitcast(F32R), AA))
                step(e.tensor_tensor(AAL, AA, AAH, ALU.subtract))
                for b in range(3, CB):
                    conv(b)

                def make_ar(c):
                    if c == 0:
                        e.wait_ge(S["ip"], 2 * NB)
                        for n in range(4):
                            e.wait_ge(S[f"wl{n}"], 1)
                    if c >= 2:
                        e.wait_ge(S["de"], c - 1)
                    e.tensor_tensor(ar_hi[c % 2], repeat(upto, NH), spread(AAH[:, c * NH:(c + 1) * NH], P),
                                    ALU.mult).then_inc(S["ar"], 1)

                make_ar(0)
                for i in range(NT + 4):
                    if i >= 4:
                        c = i - 4
                        e.wait_ge(S["O"], c + 1)
                        e.tensor_scalar(VE[:, c:c + 1], bank(6 + c % 2)[:, D:D + 1], 1.0 / INNER, 1e-5, ALU.mult,
                                        ALU.add).then_inc(S["ve"], 1)
                    c = i
                    if c + 1 < NT:
                        make_ar(c + 1)
                    if c < NT:
                        if c >= 2:
                            e.wait_ge(S["Y"], c - 1)
                        e.wait_ge(S["bt"], c + 1)
                        if c:
                            e.wait_ge(S["wt"], c)
                        e.tensor_tensor(cbm, bank(2)[:, 0:P], upto, ALU.mult).then_inc(S["cbm"], 1)
                        e.wait_ge(S["cbm"], c + 1)
                        e.wait_ge(S["L"], 2 * c + 2)
                        e.tensor_tensor(wt[c % 2], repeat(cbm, NH), Lm[c % 2], ALU.mult).then_inc(S["wt"], 1)
                        e.tensor_tensor(ce[c % 2][0:STATE], ecs[c % 2][0:STATE], repeat(bcT[0:STATE, 1, tile(c)], NH),
                                        ALU.mult).then_inc(S["ce"], 1)
                    if 2 <= i < NT + 2:
                        c = i - 2
                        e.wait_ge(S["ghi"], c + 1)
                        e.tensor_tensor(g_lo, gy[c % 2], f32(g_hi), ALU.subtract).then_inc(S["glo"], 1)
                    if 1 <= i <= NT:
                        c = i - 1
                        new = st[(c + 1) % 2][0:STATE]
                        if c < NT - 1:
                            if c:
                                e.tensor_tensor(st_t[0:STATE], st[c % 2][0:STATE],
                                                ecs[c % 2][0:STATE, :, P - 1:P].broadcast_to([STATE, NH, P]),
                                                ALU.mult).then_inc(S["st1"], 1)
                                e.wait_ge(S["st1"], c)
                            e.wait_ge(S["St"], c + 1)
                            add = bank(5)[0:STATE, :].rearrange("p (h l) -> p h l", h=NH)
                            if c:
                                e.wait_ge(S["Y"], c)
                                e.tensor_tensor(new, add, st_t[0:STATE], ALU.add).then_inc(S["st"], 1)
                            else:
                                e.tensor_copy(new, add).then_inc(S["st"], 1)
                        e.wait_ge(S["Y"], c + 1)
                        if c >= 2:
                            e.wait_ge(S["glo"], c - 1)
                            e.wait_ge(S["g2"], c - 1)
                        e.wait_ge(S["xd"], NH - 1)
                        e.wait_ge(S["xda"], 1)
                        e.tensor_tensor(gy[c % 2], bank(4).rearrange("p (h l) -> p h l", h=NH), xsD[:, :, tile(c)],
                                        ALU.add).then_inc(S["y"], 1)
                    if i == NT + 3:
                        early(phase, "logits_copy0", e)
                    if i >= 4:
                        c = i - 4
                        e.wait_ge(S["ri"], c + 1)
                        e.scalar_tensor_tensor(out=x[:, c, :], in0=bank(6 + c % 2)[:, 0:D], scalar=RI[:, c:c + 1],
                                               in1=x[:, c, :], op0=ALU.mult, op1=ALU.add).then_inc(S["fin"], 1)
                        early(phase, "stats", e, c)
                        if c == HT - 1:
                            early(phase, "veps0", e)
                    if i == NT:
                        early(phase, "norm0", e)
                    if i == NT + 1:
                        early(phase, "lo0", e)

            def pool(e):
                before["free"](e)
                for n in range(2):
                    i = e.memset(xr[n][:, 0:CONV - 1], 0.0)
                i.then_inc(S["pad"], 1)
                ln["rstd"](e, 1)
                e.wait_ge(S["raw"], 16 * 4)
                for h in range(NH):
                    o = M_OUT + h * D
                    e.tensor_scalar(m_raw[:, o:o + D], m_raw[:, o:o + D], par[:, PR_NW + h:PR_NW + h + 1], None,
                                    ALU.mult).then_inc(S["nw"], 1)
                w_lo(e, 3)

                def make_ar_lo(c):
                    if c == 0:
                        e.wait_ge(S["dt_dve"], DT_DONE)
                    else:
                        e.wait_ge(S["de"], c)
                    e.tensor_tensor(ar_lo, repeat(upto, NH), spread(AAL[:, c * NH:(c + 1) * NH], P),
                                    ALU.mult).then_inc(S["arl"], 1)

                make_ar_lo(0)
                for h in range(NH - 1):
                    e.wait_ge(S["sl"], h + 3)
                    e.tensor_scalar(xsD[:, h, :], xs[:, h, :], par[:, PR_D + h:PR_D + h + 1], None,
                                    ALU.mult).then_inc(S["xd"], 1)
                for i in range(NT + 4):
                    if i == NT:
                        early(phase, "rstd0", e)
                    if i >= 4:
                        c = i - 4
                        e.wait_ge(S["ve"], c + 1)
                        e.tensor_tensor(RI[:, c:c + 1], VE[:, c:c + 1], minus_half[:, 0:1], ALU.pow).then_inc(S["ri"], 1)
                    if i + 1 < NT:
                        make_ar_lo(i + 1)
                    c = i
                    if c < NT - 1:
                        e.wait_ge(S["X"], c + 1)
                        e.wait_ge(S["L"], 2 * c + 2)
                        if c >= 2:
                            e.wait_ge(S["St"], c - 1)
                        e.tensor_tensor(xdd[c % 2], xd[c % 2], Lm[c % 2][:, :, P - 1:P].broadcast_to([P, NH, P]),
                                        ALU.mult).then_inc(S["xdd"], 1)
                    if 2 <= i < NT + 2:
                        c = i - 2
                        q = g2[c % 2]
                        e.wait_ge(S["g2"], c + 1)
                        e.tensor_tensor(q[:, 0:2, :], q[:, 0:2, :], q[:, 2:4, :], ALU.add).then_inc(S["gs"], 1)
                        e.wait_ge(S["gs"], 2 * c + 1)
                        e.tensor_tensor(q[:, 0, :], q[:, 0, :], q[:, 1, :], ALU.add).then_inc(S["gs"], 1)
                    if 1 <= i <= NT:
                        c = i - 1
                        e.wait_ge(S["y"], c + 1)
                        e.tensor_tensor(gy[c % 2], gy[c % 2], zs[:, :, tile(c)], ALU.mult).then_inc(S["g"], 1)

            def banks_free(e):
                e.wait_ge(S["L"], 2 * NT)
                e.wait_ge(S["st"], NT - 1)

            def banks_free2(e):
                e.wait_ge(S["cbm"], NT)
                e.wait_ge(S["bt"], NT)
                e.wait_ge(S["y"], NT)

            phase.update(early_stages(ln))
            phase.update(w_hi0=lambda e: w_hi(e, 0), w_lo0=lambda e: w_lo(e, 0), in_proj0=in_proj0)
            phase.update(sync=sync, pe=pe, act=act, dve=dve, pool=pool, spare=5, banks_free=banks_free,
                         banks_free2=banks_free2, us_free=lambda e: e.wait_ge(S["y"], NT),
                         x_ready=lambda e, t: e.wait_ge(S["fin"], t + 1),
                         xt_free=lambda e, h: e.wait_ge(S["ip"], 2 * NB),
                         free=lambda e: e.wait_ge(S["fin"], NT))
            return phase

        att = attention()
        chain = [att]
        if phases >= 2:
            chain.append(ffn("f0", True, chain[-1]))
        if phases >= 3:
            chain.append(mixer(chain[-1]))
        if phases >= 4:
            chain.append(ffn("f1", False, chain[-1]))
        for front, behind in zip(chain, chain[1:]):
            front["next"].update(behind)

        block = ctx.enter_context(nc.Block())

        @block.sync
        def _(e):
            for h in range(2):
                rows = ins["x"][HALF * h:HALF * h + HALF, :].rearrange("(t p) d -> p t d", p=P)
                e.dma_start(x[:, HT * h:HT * h + HT, :], rows).then_inc(s_x[h], 16)
                if h == 0:
                    e.dma_start(cf, ins["cf"]).then_inc(s_cf, 16)
            for ph in chain:
                ph["sync"](e)
            last = chain[-1]
            for t in range(0, NT, 2):
                last["x_ready"](e, t + 1)
                rows = out[P * t:P * (t + 2), :].rearrange("(t p) d -> p t d", p=P)
                e.dma_start(rows, x[:, t:t + 2, :]).then_inc(s_out, 16)
            e.wait_ge(s_out, 16 * NT // 2)

        @block.tensor
        def _(e):
            for n, ph in enumerate(chain):
                if n == 1:
                    e.wait_ge(s_par, 16)
                ph["pe"](e)

        @block.scalar
        def _(e):
            for n, ph in enumerate(chain):
                if n == 2:
                    e.wait_ge(s_par, 16)
                ph["act"](e)

        @block.vector
        def _(e):
            for n, ph in enumerate(chain):
                if n == 1:
                    e.wait_ge(s_par, 16)
                    e.wait_ge(s_cf, 16)
                ph["dve"](e)

        @block.gpsimd
        def _(e):
            for ph in chain:
                ph["pool"](e)


def constants():
    r, c = np.arange(P)[:, None], np.arange(P)[None, :]
    cf = np.concatenate([r == c, r > c, r <= c, np.ones((P, P))], 1)
    m0 = (c <= r) & ((c < SINK) | (c >= r - WINDOW + 1))
    k = np.arange(NKEY)[None, :]
    w = k - SINK - WINDOW
    m1 = (k < SINK) | ((w <= r) & (w >= r - WINDOW + 1))
    drop = lambda m, n: np.tile(np.where(m, 0.0, MASKED), (1, n))
    cb = np.concatenate([r == c, np.broadcast_to(c // RANK, (P, P)), drop(m0, GROUP), drop(m1, GROUP)], 1)
    bits = cb.astype(np.float32).view(np.uint32) >> 16
    return cf.astype(np.float32), bits.astype(np.uint16)


def pack(i):
    a = {k.removeprefix("L0_"): np.asarray(v) for k, v in i.items()}
    f = np.float32
    kmaj = lambda w: w.T.reshape(-1, P, w.shape[0]).transpose(1, 0, 2)
    flat = lambda w: np.ascontiguousarray(w.reshape(P, -1))
    padh = lambda w, ax: np.concatenate(
        [w, np.zeros([HIDP - HID if n == ax else s for n, s in enumerate(w.shape)], f)], ax)
    er = lambda w: w.reshape(ER, w.shape[2])
    eb = lambda w: w.transpose(0, 2, 1).reshape(ER, w.shape[1])
    wq, wo = a["attn_a_wq"], a["attn_a_wo"]
    gw = GROUP * HD
    blocks = lambda w, n: [w[..., b * n:(b + 1) * n] for b in range(HB)]
    per_block = zip(blocks(kmaj(padh(a["ffn_w_up"], 0)), P), blocks(kmaj(padh(a["ffn_w_gate"], 0)), P),
                    blocks(padh(eb(a["ffn_up_B"]), 1), P), blocks(padh(eb(a["ffn_gate_B"]), 1), P),
                    kmaj(padh(a["ffn_w_down"], 1)).transpose(1, 0, 2),
                    kmaj(padh(er(a["ffn_down_A"]), 1)).transpose(1, 0, 2))
    ffn = [kmaj(er(a["ffn_up_A"])), kmaj(er(a["ffn_gate_A"]))] + [w for b in per_block for w in b] + [eb(a["ffn_down_B"])]
    ip = a["attn_b_in_proj_w"]
    z, xbc, dt = ip[:INNER], ip[INNER:2 * INNER + 2 * STATE], ip[2 * INNER + 2 * STATE:]
    B, C = slice(INNER, INNER + STATE), slice(INNER + STATE, INNER + 2 * STATE)
    fill = lambda w: np.concatenate([w, np.zeros((P - w.shape[0],) + w.shape[1:], f)])
    order = lambda w, dt: np.concatenate([w[C], w[B], fill(dt), w[:INNER]])
    cw, cbias = order(a["attn_b_conv_w"], np.zeros((0, CONV), f)), order(a["attn_b_conv_b"], np.zeros(0, f))
    row = lambda v: np.broadcast_to(v[None, :], (P, v.shape[0]))
    par = [cw.reshape(CB, P, CONV).transpose(1, 0, 2), cbias.reshape(CB, P).T,
           a["attn_b_norm_w"].reshape(NH, P).T, row(a["attn_b_D"]), row(a["attn_b_dt_bias"]), row(a["attn_b_A_log"]),
           kmaj(a["ffn_gate_w"])]
    cf, cb = constants()
    return {
        "x": a["attn_a_x"].reshape(T, D), "cf": cf, "cb": cb,
        "par": np.concatenate([flat(np.ascontiguousarray(p)) for p in par], 1),
        "wk": flat(kmaj(a["attn_a_wk"])), "wv": flat(kmaj(a["attn_a_wv"])),
        "wq": np.stack([flat(kmaj(wq[g * gw:(g + 1) * gw])) for g in range(KV)]),
        "wo": np.stack([flat(kmaj(wo[:, g * gw:(g + 1) * gw])) for g in range(KV)]),
        "ffn": np.concatenate([flat(p) for p in ffn], 1),
        "ssd": np.concatenate([flat(kmaj(np.concatenate([order(xbc, dt), z])).reshape(P, KB, -1, P).transpose(0, 2, 1, 3)), flat(kmaj(a["attn_b_out_proj_w"]))], 1),
    }


def kernel(**inputs):
    import concourse.bacc as bacc
    from concourse.bass_utils import run_bass_kernel_spmd

    nc = bacc.Bacc("TRN2", target_bir_lowering=False, num_devices=1)
    arrays = {f"in_{k}": np.ascontiguousarray(v) for k, v in pack(inputs).items()}
    ins = {k[3:]: nc.dram_tensor(k, v.shape, mybir.dt.from_np(v.dtype), kind="ExternalInput").ap()
           for k, v in arrays.items()}
    out = nc.dram_tensor("out_x", (T, D), F32, kind="ExternalOutput").ap()
    build(nc, ins, out)
    r = run_bass_kernel_spmd(nc, [arrays], core_ids=[0])
    return r.results[0]["out_x"].reshape(1, T, D)
```
